# Optimizing a Trainium2 kernel written in Bass

```python
import numpy as np
import jax
import jax.numpy as jnp

def _softmax(x, axis=-1):
    return jax.nn.softmax(x, axis=axis)

def _gelu(x):
    return jax.nn.gelu(x, approximate=True)

def _silu(x):
    return jax.nn.silu(x)

def _sigmoid(x):
    return jax.nn.sigmoid(x)

def _layernorm(x, axis=-1, eps=1e-05):
    m = jnp.mean(x, axis=axis, keepdims=True)
    v = jnp.var(x, axis=axis, keepdims=True)
    return (x - m) / jnp.sqrt(v + eps)

def _scatter_add(tgt, idx, src, axis=0):
    return tgt.at[idx].add(src)

def _segment_sum(src, seg, n):
    return jax.ops.segment_sum(src, seg, n)
kernel_name = 'mk_adj_preln_d4_adj_r2_3c8ec2'

def setup_inputs(seed: int=0):
    np.random.seed(seed)
    _w = jnp.asarray

    def _rec_inputs():
        import jax
        import jax.numpy as jnp
        _gk = jax.random.key(seed)
        x = -0.0001546 + 1 * jax.random.normal(jax.random.fold_in(_gk, 1), (128, 128, 128), jnp.float32)
        _a = jax.random.bernoulli(jax.random.fold_in(_gk, 2), 0.03125, (128, 128))
        _a = jnp.logical_or(_a, jnp.swapaxes(_a, -1, -2))
        _a = jnp.logical_or(_a, jnp.eye(128, dtype=bool))
        _af = _a.astype(jnp.float32)
        _af = _af * jax.random.uniform(jax.random.fold_in(_gk, 3), (128, 128), jnp.float32, 0.05, 0.999927)
        adj = _af
        return (x, adj)
    x, adj = _rec_inputs()

    def _L0_gnn_setup():
        import jax, jax.numpy as jnp
        import numpy as np
        B, N, D = (2048, 128, 128)
        key = jax.random.key(seed)
        ks = jax.random.split(key, 6)
        return {'label': jax.random.normal(ks[0], (B, N, D), dtype=jnp.float32), 'adj_in': jax.random.uniform(ks[1], (N, N), dtype=jnp.float32), 'adj_out': jax.random.uniform(ks[2], (N, N), dtype=jnp.float32), 'edge_bias': jnp.zeros((N, D), dtype=jnp.float32), 'gate_weight': jax.random.normal(ks[3], (D, 1), dtype=jnp.float32) * (6.0 / (D + 1)) ** 0.5, 'bias_gate': jnp.zeros((N, 1), dtype=jnp.float32), 'out_edge_bias': jnp.zeros((N, D), dtype=jnp.float32), 'out_gate_weight': jax.random.normal(ks[4], (D, 1), dtype=jnp.float32) * (6.0 / (D + 1)) ** 0.5, 'out_bias_gate': jnp.zeros((N, 1), dtype=jnp.float32), 'loop_gate': jax.random.normal(ks[5], (D, 1), dtype=jnp.float32) * (6.0 / (D + 1)) ** 0.5}
    _L0_gnn_all = _L0_gnn_setup()
    _L0_gnn_in = {k: v for k, v in _L0_gnn_all.items() if k in ('edge_bias', 'gate_weight', 'bias_gate', 'out_edge_bias', 'out_gate_weight', 'out_bias_gate', 'loop_gate')}
    del _L0_gnn_all

    def _L1_gnn_setup():
        import jax, jax.numpy as jnp
        import numpy as np
        B, J, F_IN, F_OUT = (8192, 17, 128, 128)
        key = jax.random.key(seed)
        k1, k2, k3, k4 = jax.random.split(key, 4)
        gain = 1.414
        bound = gain * np.sqrt(6.0 / (F_IN + F_OUT))
        W = jax.random.uniform(k2, (3, F_IN, F_OUT), dtype=jnp.float32, minval=-bound, maxval=bound)
        stdv = 1.0 / np.sqrt(F_OUT)
        bias = jax.random.uniform(k4, (F_OUT,), dtype=jnp.float32, minval=-stdv, maxval=stdv)
        return {'x': jax.random.normal(k1, (B, J, F_IN), dtype=jnp.float32), 'W': W, 'adj': jax.random.uniform(k3, (J, J), dtype=jnp.float32), 'bias': bias}
    _L1_gnn_all = _L1_gnn_setup()
    _L1_gnn_in = {k: v for k, v in _L1_gnn_all.items() if k in ('W', 'bias')}
    del _L1_gnn_all

    def _L2_gnn_setup():
        import jax, jax.numpy as jnp
        import numpy as np
        B, T, D, H = (64, 1024, 128, 128)
        MAX_SKIP = 4

        def _lstm_last(Wih, Whh, bih, bhh, xs):
            N, _, Hd = xs.shape
            bias = bih + bhh

            def step(carry, x_t):
                h, c = carry
                g = x_t @ Wih.T + h @ Whh.T + bias
                i, f, gg, o = jnp.split(g, 4, axis=-1)
                c = jax.nn.sigmoid(f) * c + jax.nn.sigmoid(i) * jnp.tanh(gg)
                h = jax.nn.sigmoid(o) * jnp.tanh(c)
                return ((h, c), None)
            init = (jnp.zeros((N, Hd), xs.dtype), jnp.zeros((N, Hd), xs.dtype))
            (h_last, _), _ = jax.lax.scan(step, init, jnp.swapaxes(xs, 0, 1))
            return h_last
        key = jax.random.key(seed)
        ks = jax.random.split(key, 8)
        s = 0.05
        x = jax.random.normal(ks[0], (B, T, D), jnp.float32)
        adj = jax.random.uniform(ks[1], (T, T), jnp.float32) / T
        Wg0 = jax.random.normal(ks[2], (D, H), jnp.float32) * s
        bg0 = jnp.zeros((H,), jnp.float32)
        Wg1 = jax.random.normal(ks[3], (H, H), jnp.float32) * s
        bg1 = jnp.zeros((H,), jnp.float32)
        Wih = jax.random.normal(ks[4], (MAX_SKIP, 4 * H, H), jnp.float32) * s
        Whh = jax.random.normal(ks[5], (MAX_SKIP, 4 * H, H), jnp.float32) * s
        bih = jax.random.normal(ks[6], (MAX_SKIP, 4 * H), jnp.float32) * s
        bhh = jax.random.normal(ks[7], (MAX_SKIP, 4 * H), jnp.float32) * s
        return dict(x=x, adj=adj, Wg0=Wg0, bg0=bg0, Wg1=Wg1, bg1=bg1, Wih=Wih, Whh=Whh, bih=bih, bhh=bhh)
    _L2_gnn_all = _L2_gnn_setup()
    _L2_gnn_in = {k: v for k, v in _L2_gnn_all.items() if k in ('Wg0', 'bg0', 'Wg1', 'bg1', 'Wih', 'Whh', 'bih', 'bhh')}
    del _L2_gnn_all

    def _L3_gnn_setup():
        import jax, jax.numpy as jnp
        import numpy as np
        ALPHA = 0.2
        key = jax.random.key(seed)
        k1, k2, k3, k4 = jax.random.split(key, 4)
        B, N, Fin, Fout = (8, 1024, 128, 128)
        h = jax.random.normal(k1, (B, N, Fin), dtype=jnp.float32)
        adj = jax.random.randint(k2, (N, N), 0, 2).astype(jnp.float32)
        adj = jnp.maximum(adj, jnp.eye(N, dtype=jnp.float32))

        def xavier(k, shape, gain=1.414):
            fan_in, fan_out = (shape[0], shape[1])
            a = gain * np.sqrt(6.0 / (fan_in + fan_out))
            return jax.random.uniform(k, shape, dtype=jnp.float32, minval=-a, maxval=a)
        W = xavier(k3, (Fin, Fout))
        a = xavier(k4, (2 * Fout, 1))
        return {'h': h, 'adj_matrix': adj, 'W': W, 'a': a}
    _L3_gnn_all = _L3_gnn_setup()
    _L3_gnn_in = {k: v for k, v in _L3_gnn_all.items() if k in ('W', 'a')}
    del _L3_gnn_all
    return {'x': x, 'adj': adj, 'L0_gnn_edge_bias': _L0_gnn_in['edge_bias'], 'L0_gnn_gate_weight': _L0_gnn_in['gate_weight'], 'L0_gnn_bias_gate': _L0_gnn_in['bias_gate'], 'L0_gnn_out_edge_bias': _L0_gnn_in['out_edge_bias'], 'L0_gnn_out_gate_weight': _L0_gnn_in['out_gate_weight'], 'L0_gnn_out_bias_gate': _L0_gnn_in['out_bias_gate'], 'L0_gnn_loop_gate': _L0_gnn_in['loop_gate'], 'L1_gnn_W': _L1_gnn_in['W'], 'L1_gnn_bias': _L1_gnn_in['bias'], 'L2_gnn_Wg0': _L2_gnn_in['Wg0'], 'L2_gnn_bg0': _L2_gnn_in['bg0'], 'L2_gnn_Wg1': _L2_gnn_in['Wg1'], 'L2_gnn_bg1': _L2_gnn_in['bg1'], 'L2_gnn_Wih': _L2_gnn_in['Wih'], 'L2_gnn_Whh': _L2_gnn_in['Whh'], 'L2_gnn_bih': _L2_gnn_in['bih'], 'L2_gnn_bhh': _L2_gnn_in['bhh'], 'L3_gnn_W': _L3_gnn_in['W'], 'L3_gnn_a': _L3_gnn_in['a']}

def reference(x, adj, L0_gnn_edge_bias, L0_gnn_gate_weight, L0_gnn_bias_gate, L0_gnn_out_edge_bias, L0_gnn_out_gate_weight, L0_gnn_out_bias_gate, L0_gnn_loop_gate, L1_gnn_W, L1_gnn_bias, L2_gnn_Wg0, L2_gnn_bg0, L2_gnn_Wg1, L2_gnn_bg1, L2_gnn_Wih, L2_gnn_Whh, L2_gnn_bih, L2_gnn_bhh, L3_gnn_W, L3_gnn_a):
    import jax
    import jax.numpy as jnp

    def _L0_gnn_ref(label, adj_in, adj_out, edge_bias, gate_weight, bias_gate, out_edge_bias, out_gate_weight, out_bias_gate, loop_gate):
        import jax, jax.numpy as jnp
        import numpy as np
        B, N, D = (2048, 128, 128)
        h = label
        origin = jax.lax.stop_gradient(jnp.where(adj_in <= 0, adj_in, 1.0))
        h_in = jnp.einsum('mn,bnd->bmd', origin * adj_in, h)
        in_gate = jnp.einsum('bnd,do->bno', h, gate_weight) + bias_gate
        msg_in = (h_in + edge_bias) * jax.nn.sigmoid(in_gate)
        h_out = jnp.einsum('mn,bnd->bmd', origin.T * adj_out, h)
        out_gate = jnp.einsum('bnd,do->bno', h, out_gate_weight) + out_bias_gate
        msg_out = (h_out + out_edge_bias) * jax.nn.sigmoid(out_gate)
        lp_gate = jnp.einsum('bnd,do->bno', h, loop_gate)
        msg_loop = h * jax.nn.sigmoid(lp_gate)
        return jax.nn.relu(msg_in + msg_out + msg_loop)

    def _L1_gnn_ref(x, W, adj, bias):
        import jax, jax.numpy as jnp
        import numpy as np
        B, J, F_IN, F_OUT = (8192, 17, 128, 128)
        adj_0 = jnp.diag(jnp.diagonal(adj))
        adj_1 = jnp.triu(adj, k=1)
        adj_2 = jnp.tril(adj, k=-1)
        h = jnp.einsum('bjf,kfo->kbjo', x, W)
        out = jnp.einsum('ij,bjo->bio', adj_0, h[0]) + jnp.einsum('ij,bjo->bio', adj_1, h[1]) + jnp.einsum('ij,bjo->bio', adj_2, h[2])
        return out + bias[None, None, :]

    def _L2_gnn_ref(x, adj, Wg0, bg0, Wg1, bg1, Wih, Whh, bih, bhh):
        import jax, jax.numpy as jnp
        import numpy as np
        B, T, D, H = (64, 1024, 128, 128)
        MAX_SKIP = 4

        def _lstm_last(Wih, Whh, bih, bhh, xs):
            N, _, Hd = xs.shape
            bias = bih + bhh

            def step(carry, x_t):
                h, c = carry
                g = x_t @ Wih.T + h @ Whh.T + bias
                i, f, gg, o = jnp.split(g, 4, axis=-1)
                c = jax.nn.sigmoid(f) * c + jax.nn.sigmoid(i) * jnp.tanh(gg)
                h = jax.nn.sigmoid(o) * jnp.tanh(c)
                return ((h, c), None)
            init = (jnp.zeros((N, Hd), xs.dtype), jnp.zeros((N, Hd), xs.dtype))
            (h_last, _), _ = jax.lax.scan(step, init, jnp.swapaxes(xs, 0, 1))
            return h_last
        h = jax.nn.relu(jnp.einsum('ts,bsh->bth', adj, x @ Wg0 + bg0))
        h = jax.nn.relu(jnp.einsum('ts,bsh->bth', adj, h @ Wg1 + bg1))
        Bv, Tv, Hd = h.shape
        for p in range(1, MAX_SKIP + 1):
            nw = Tv // p
            wins = h[:, :nw * p, :].reshape(Bv * nw, p, Hd)
            last = _lstm_last(Wih[p - 1], Whh[p - 1], bih[p - 1], bhh[p - 1], wins)
            idx = jnp.arange(nw) * p + (p - 1)
            h = h.at[:, idx, :].set(last.reshape(Bv, nw, Hd))
        return h

    def _L3_gnn_ref(h, adj_matrix, W, a):
        import jax, jax.numpy as jnp
        import numpy as np
        ALPHA = 0.2
        Fout = W.shape[1]
        Wh = jnp.einsum('bnf,fo->bno', h, W)
        a1, a2 = (a[:Fout, 0], a[Fout:, 0])
        s1 = Wh @ a1
        s2 = Wh @ a2
        e = s1[:, :, None] + s2[:, None, :]
        e = jnp.where(e >= 0, e, ALPHA * e)
        e = jnp.where(adj_matrix[None] == 0, -jnp.inf, e)
        attention = jax.nn.softmax(e, axis=-1)
        h_prime = jnp.einsum('bij,bjo->bio', attention, Wh)
        return h_prime
    h = jnp.maximum(_layernorm(x, axis=-1), 0.0)
    x = x + _L0_gnn_ref(h, adj, adj, L0_gnn_edge_bias, L0_gnn_gate_weight, L0_gnn_bias_gate, L0_gnn_out_edge_bias, L0_gnn_out_gate_weight, L0_gnn_out_bias_gate, L0_gnn_loop_gate)
    h = jnp.maximum(_layernorm(x, axis=-1), 0.0)
    x = x + _L1_gnn_ref(h, L1_gnn_W, adj, L1_gnn_bias)
    h = jnp.maximum(_layernorm(x, axis=-1), 0.0)
    x = x + _L2_gnn_ref(h, adj, L2_gnn_Wg0, L2_gnn_bg0, L2_gnn_Wg1, L2_gnn_bg1, L2_gnn_Wih, L2_gnn_Whh, L2_gnn_bih, L2_gnn_bhh)
    h = jnp.maximum(_layernorm(x, axis=-1), 0.0)
    x = x + _L3_gnn_ref(h, adj, L3_gnn_W, L3_gnn_a)
    return x

_drawn_inputs = setup_inputs


def setup_inputs(seed=0):
    import zlib

    import numpy as np

    out = dict(_drawn_inputs(seed))
    spreads = {'L0_gnn_edge_bias': (0.0, 0.446),
     'L0_gnn_bias_gate': (0.0, 0.71),
     'L0_gnn_out_edge_bias': (0.0, 0.459),
     'L0_gnn_out_bias_gate': (0.0, 0.674),
     'L2_gnn_bg0': (0.0, 0.8),
     'L2_gnn_bg1': (0.0, 2.0)}
    factors = {'L1_gnn_bias': 4.342,
     'L2_gnn_Wg0': 3.409,
     'L2_gnn_Whh': 8.0,
     'L2_gnn_bih': 8.0,
     'L2_gnn_bhh': 8.0}
    for name, (base, spread) in spreads.items():
        noise = np.random.default_rng([zlib.crc32(name.encode()), seed]).standard_normal(out[name].shape)
        drawn = base * np.exp(spread * noise) if base else spread * noise
        out[name] = jnp.asarray(drawn.astype(out[name].dtype))
    for name, factor in factors.items():
        out[name] = (out[name] * factor).astype(out[name].dtype)
    return out
```

```python
from contextlib import ExitStack

import concourse.bass as bass
from concourse import mybir

F32 = mybir.dt.float32
BF16 = mybir.dt.bfloat16
ALU = mybir.AluOpType
ACT = mybir.ActivationFunctionType
AX_X = mybir.AxisListType.X

P = 128
GB = 4
CHAINS = 2
COLS = GB * P
MAX_SKIP = 4
EPS = 1e-5
ALPHA = 0.2
MASKED = -float(2 ** 100)
I, F, G, O = range(4)

LSTM_STEPS = [(p, s) for p in range(1, MAX_SKIP + 1) for s in range(p)]


def _lstm_names():
    pe, act, dve = [], [], []
    for p, s in LSTM_STEPS:
        at = f"{p}.{s}"
        if p == 1:
            pe += [at + "i", at + "g", at + "o"]
            act += [at + "i", at + "g", at + "o", at + "tc"]
            dve += [at + "c", at + "h"]
        else:
            pe += [at + "ig", at + "fo"]
            act += [at + "i", at + "g"] + ([at + "f"] if s else []) + [at + "o", at + "tc"]
            dve += ([at + "ig", at + "fc"] if s else []) + [at + "c", at + "h"]
    return pe, act, dve


ROUND = 10000
LAG = 5001
PLACES = {
    "pe": {
        "front": {2: -5149, 3: -4798, 4: -4026, 8: -2146, 9: -2083, 10: -1866, 12: -613, 13: -250, 14: 17, 15: 247},
        "lstm": {0: 578, 1: 930, 2: 2036, 3: 2572, 4: 3044, 6: 3821, 7: 4275, 8: 5277, 9: 5590, 10: 5725, 12: 6313,
                 13: 7507, 14: 7638, 15: 8302, 16: 8323, 17: 9015, 18: 9739},
        "att": {0: 10454, 2: 11111, 3: 11470, 4: 12233, 6: 13646, 7: 14163},
    },
    "act": {
        "front": {1: -5101, 2: -4584, 3: -4479, 4: -3891, 7: -1876, 8: -1871, 9: -1609, 11: -377, 13: 185, 15: 676},
        "lstm": {0: 1411, 1: 1822, 2: 2257, 3: 3076, 4: 3438, 5: 3742, 6: 4244, 7: 4262, 8: 5799, 9: 5947,
                 10: 6528, 11: 6854, 12: 7044, 13: 7792, 14: 8329, 15: 8435, 16: 8910, 17: 9498, 18: 9679, 19: 10497},
        "att": {1: 11941, 2: 11987, 3: 12136, 5: 13529, 6: 14126},
    },
    "dve": {
        "front": {0: -7725, 1: -6753, 3: -6135, 4: -5915, 5: -4499, 6: -4422, 7: -3298, 8: -3249, 9: -2799,
                  10: -2451, 11: -2035, 12: -1730, 14: -1555},
        "lstm": {0: 33, 1: 558, 2: 785, 3: 1783, 4: 2284, 5: 2466, 6: 2891, 7: 3238, 8: 4199, 9: 4316, 10: 5160,
                 11: 5287, 12: 5648, 13: 6387, 14: 7027, 15: 7289, 16: 7770, 17: 8250, 18: 8794, 19: 9155},
        "att": {0: 9827, 1: 10235, 3: 11125, 4: 11707, 7: 13339},
    },
    "pool": {
        "front": {0: -11277, 4: -10177, 5: -8106, 6: -6612, 10: -6425},
        "lstm": {3: -2396},
        "att": {0: 6580},
    },
}
_LPE, _LACT, _LDVE = _lstm_names()

STEPS = {
    "front": {
        "pe": ["hT", "gates", "in", "out", "z0", "z1", "z2", "z3", "sem", "q", "w0", "w1", "w2"],
        "act": ["h0", "hT", "tanh", "e2", "h1", "z0", "z2", "h2", "y0", "hin"],
        "dve": ["st0", "sv0", "d0", "dd0", "m20", "mv0", "xn0", "gz", "g", "u1", "u2", "u", "s", "x1", "st1", "sv1", "d1", "dd1", "m21", "mv1", "xn1", "z1", "z3",
                "x2", "st2", "sv2", "d2", "dd2", "m22", "mv2", "xn2", "q", "y1"],
        "pool": ["rs0", "e0", "e1", "e01", "e", "rs1", "x1b", "rs2"],
    },
    "lstm": {"pe": _LPE, "act": _LACT, "dve": _LDVE, "pool": ["hold"]},
    "att": {
        "pe": ["h", "hT", "wh01", "wh23", "z", "aT", "num01", "num23"],
        "act": ["h3", "hT", "wh", "p", "aT"],
        "dve": ["x3", "st", "sv", "d", "dd", "m2", "mv", "xn", "wh", "ee", "lr", "n0", "nm", "r01", "r23", "out"],
        "pool": ["rs"],
    },
}


def graph_layers_kernel(nc, x, adj, adj_t, edge_bias, out_edge_bias, gate_vecs, gate_biases, sem_w, rows,
                        gcn_w, wih_t, whh_t, lstm_b, att_w, out):
    B, N, D = x.shape
    assert N == P and D == P and B % (GB * CHAINS) == 0
    ROUNDS = B // (GB * CHAINS)
    assert ROUNDS >= 4

    ctx = ExitStack()
    with ctx:
        def sb(name, shape, dt=F32):
            return ctx.enter_context(nc.sbuf_tensor(name, [P] + shape, dt))

        def per_chain(name, shape, dt=F32):
            return [sb(f"{name}_{c}", shape, dt) for c in range(CHAINS)]

        def sem(name):
            return ctx.enter_context(nc.semaphore(name))

        adj_n = sb("adj_n", [P])
        adjT = sb("adjT", [P])
        a_in = sb("a_in", [P])
        a_out = sb("a_out", [P])
        a_sem = sb("a_sem", [3, P])
        org = sb("org", [P])
        eb = sb("eb", [P])
        oeb = sb("oeb", [P])
        gvec = sb("gvec", [3])
        gbias = sb("gbias", [3])
        semW = sb("semW", [3, P])
        rows_t = sb("rows_t", [4, P])
        bg0_row = sb("bg0_row", [P])
        rows_bc = sb("rows_bc", [4, P])
        Wg = sb("Wg", [2, P])
        WihT = sb("WihT", [MAX_SKIP, 4 * P])
        WhhT = sb("WhhT", [MAX_SKIP - 1, 4 * P])
        lb = sb("lb", [2, MAX_SKIP, 4])
        gb = sb("gb", [MAX_SKIP, 4])
        attW = sb("attW", [P + 2])
        wa2 = sb("wa2", [1])
        wa2_bc = sb("wa2_bc", [P])
        scr = sb("scr", [P])
        ident = sb("ident", [P])
        identb = sb("identb", [P], BF16)
        ones = sb("ones", [P])
        zero = sb("zero", [P])
        maskb = sb("maskb", [P], BF16)
        half = sb("half", [GB])
        rsum = sb("rsum", [P])
        part = sb("part", [2, 3, P], BF16)
        rest = sb("rest", [2, P])
        pairs_row = sb("pairs_row", [2, 9, P], BF16)
        bg0_9 = sb("bg0_9", [P], BF16)
        rs_9 = sb("rs_9", [P], BF16)

        xin = per_chain("xin", [GB, P])
        st = per_chain("st", [GB, 6])
        mv = per_chain("mv", [GB, 7])
        rs = per_chain("rs", [GB])
        xn = per_chain("xn", [GB, P])
        h = per_chain("h", [GB, P])
        hT = per_chain("hT", [GB, P])
        gz = per_chain("gz", [GB, 3])
        gt = per_chain("gt", [GB, 3])
        gg = per_chain("gg", [GB, 3])
        e0 = per_chain("e0", [GB, P])
        e1 = per_chain("e1", [GB, P])
        e2 = per_chain("e2", [GB, P])
        u1 = per_chain("u1", [GB, P])
        u2 = per_chain("u2", [GB, P])
        x1 = per_chain("x1", [GB, P])
        x1b = per_chain("x1b", [GB, P])
        z = per_chain("z", [GB, 3, P])
        x2 = per_chain("x2", [GB, P])
        x2h = per_chain("x2h", [GB, P])
        q = per_chain("q", [GB, P])
        y0 = per_chain("y0", [GB, P])
        y1 = per_chain("y1", [GB, P])
        hin = per_chain("hin", [GB, P])
        ti = per_chain("ti", [COLS])
        tg = per_chain("tg", [COLS])
        tf = per_chain("tf", [COLS // 2])
        to = per_chain("to", [COLS])
        c2 = per_chain("c2", [COLS])
        ig = per_chain("ig", [COLS // 2])
        fc = per_chain("fc", [COLS // 2])
        tc = per_chain("tc", [COLS])
        hs = per_chain("hs", [COLS // 2])
        H = per_chain("H", [GB, P])
        x3 = per_chain("x3", [GB, P])
        ast = per_chain("ast", [GB, 6])
        amv = per_chain("amv", [GB, 7])
        ars = per_chain("ars", [GB])
        axn = per_chain("axn", [GB, P])
        ah = per_chain("ah", [GB, P])
        ahT = per_chain("ahT", [GB, P])
        wh = per_chain("wh", [GB, P + 2])
        n0 = per_chain("n0", [GB])
        nm = per_chain("nm", [GB])
        ee = per_chain("ee", [GB, P])
        pr = per_chain("pr", [GB, P])
        aT = per_chain("aT", [GB, P])
        rc = per_chain("rc", [GB, 1])
        xo = per_chain("xo", [GB, P])

        bank = [ctx.enter_context(nc.psum_tensor(f"bank{i}", [P, COLS], F32)) for i in range(8)]
        La, Lb = [bank[0], bank[2]], [bank[1], bank[3]]
        Ra, Rb = [bank[4], bank[6]], [bank[5], bank[7]]

        sig = {(stage, eng): [sem(f"{stage}_{eng}_{c}") for c in range(CHAINS)]
               for stage in STEPS for eng in STEPS[stage]}
        x_loaded = [sem(f"x_loaded_{c}") for c in range(CHAINS)]
        out_free = [sem(f"out_free_{c}") for c in range(CHAINS)]
        const_loaded = sem("const_loaded")
        pool_const = sem("pool_const")
        dve_const = sem("dve_const")
        pe_const = sem("pe_const")
        pairs_ready = sem("pairs_ready")
        pairs_moved = sem("pairs_moved")
        consts_ready = sem("consts_ready")

        def wait(eng, stage, who, c, step, inst):
            steps = STEPS[stage][who]
            value = inst * len(steps) + (steps.index(step) + 1)
            if not (isinstance(value, int) and value <= 0):
                eng.wait_ge(sig[stage, who][c], value)

        def b3(t, c):
            return t[c][:, :].rearrange("p (b o) -> p b o", o=1).to_broadcast([P, GB, P])

        def over_b(t):
            return t.rearrange("p (o d) -> p o d", o=1).to_broadcast([P, GB, P])

        def flat(t):
            return t[:, :, :].rearrange("p b d -> p (b d)")

        def as_b(t):
            return t[:, :].rearrange("p (b d) -> p b d", d=P)

        N_CONST = 18
        N_POOL_CONST = 6 + CHAINS
        block = ctx.enter_context(nc.Block())

        LAST = ROUNDS - 1

        def run(eng, name, parts):
            def part(stage, j, c, inst):
                inner = not isinstance(inst, int)
                before = {"att": ("front", inst + 1) if inner or inst + 1 < ROUNDS else ("att", inst - 1),
                          "front": ("att", inst - 2) if inner or inst >= 2 else ("front", 0) if inst == 1 else None,
                          "lstm": None}[stage]
                parts[stage](j, c, inst, before)

            order = []
            for stage, places in PLACES[name].items():
                for j, place in places.items():
                    for c in range(CHAINS):
                        at = place + c * LAG
                        order.append((at % ROUND, at // ROUND, stage, j, c))
            order.sort()
            early, late = min(o[1] for o in order), max(o[1] for o in order)

            def a_round(r):
                for _, behind, stage, j, c in order:
                    if not isinstance(r, int) or 0 <= r - behind < ROUNDS:
                        part(stage, j, c, r - behind)

            first, end = late + 2, ROUNDS - 1 + early
            for r in range(early, first):
                a_round(r)
            with eng.Fori(first, end) as r:
                a_round(r)
            for r in range(end, ROUNDS + late):
                a_round(r)

        @block.sync
        def _(sp):
            for dst, src in (
                (adjT[:, :], adj_t), (adj_n[:, :], adj), (eb[:, :], edge_bias), (oeb[:, :], out_edge_bias),
                (gvec[:, :], gate_vecs), (gbias[:, :], gate_biases), (rows_t[0:1, 0, :], rows[0:1, :]),
                (rows_t[0:1, 1, :], rows[1:2, :]), (rows_t[0:1, 2, :], rows[2:3, :]),
                (rows_t[0:1, 3, :], rows[3:4, :]), (bg0_row[0:1, :], rows[4:5, :]),
                (semW[:, :, :], sem_w.rearrange("k f o -> f k o")),
                (Wg[:, :, :], gcn_w.rearrange("k f o -> f k o")),
                (attW[:, 0:P], att_w), (lb[:, 0, :, :], lstm_b[0]), (lb[:, 1, :, :], lstm_b[1]),
                (WihT[:, :, :], wih_t.rearrange("k d g -> d k g")),
                (WhhT[:, :, :], whh_t.rearrange("k d g -> d k g")),
            ):
                sp.dma_start(dst, src).then_inc(const_loaded, 16)

            def load(c, inst):
                wait(sp, "front", "dve", c, "x1", inst - 1)
                first = (inst * CHAINS + c) * GB
                sp.dma_start(xin[c][:, :, :], x[bass.ds(first, GB), :, :].rearrange("b n d -> n b d")
                             ).then_inc(x_loaded[c], 16)

            def store(c, inst):
                wait(sp, "att", "dve", c, "out", inst)
                first = (inst * CHAINS + c) * GB
                sp.dma_start(out[bass.ds(first, GB), :, :].rearrange("b n d -> n b d"), xo[c][:, :, :]
                             ).then_inc(out_free[c], 16)

            for c in range(CHAINS):
                sp.sem_inc(out_free[c], 16)
                load(c, 0)
            sp.wait_ge(pairs_ready, 1)
            sp.dma_start(bg0_9[0:9, :], pairs_row[0:1, 0, :, :]).then_inc(pairs_moved, 16)
            sp.dma_start(rs_9[0:9, :], pairs_row[0:1, 1, :, :]).then_inc(pairs_moved, 16)

            for c in range(CHAINS):
                load(c, 1)
            with sp.Fori(1, ROUNDS - 1) as k:
                for c in range(CHAINS):
                    load(c, k + 1)
                for c in range(CHAINS):
                    store(c, k - 1)
            for inst in (ROUNDS - 2, ROUNDS - 1):
                for c in range(CHAINS):
                    store(c, inst)
            for c in range(CHAINS):
                sp.wait_ge(out_free[c], 16 * (ROUNDS + 1))

        @block.gpsimd
        def _(pool):
            g = nc.gpsimd
            g.memset(zero[:, :], 0.0).then_inc(pool_const, 1)
            g.memset(ones[:, :], 1.0).then_inc(pool_const, 1)
            for c in range(CHAINS):
                g.memset(wh[c][:, :, P + 1:P + 2], 1.0).then_inc(pool_const, 1)
            pool.wait_ge(pool_const, 2 + CHAINS)
            g.affine_select(out=ident[:, :], in_=zero[:, :], compare_op=ALU.not_equal, fill=1.0, base=0,
                            pattern=[[-1, P]], channel_multiplier=1).then_inc(pool_const, 1)
            pool.wait_ge(const_loaded, 16 * N_CONST)
            for k, (op, sign) in enumerate(((ALU.is_equal, 1), (ALU.is_gt, 1), (ALU.is_gt, -1))):
                g.affine_select(out=a_sem[:, k, :], in_=adjT[:, :], compare_op=op, fill=0.0, base=0,
                                pattern=[[-sign, P]], channel_multiplier=sign).then_inc(pool_const, 1)
            pool.wait_ge(consts_ready, 1)

            def norm_scale(stage, mv_t, rs_t, c, inst, tag):
                wait(pool, stage, "dve", c, "mv" + tag, inst)
                g.tensor_tensor(rs_t[c][:, :], mv_t[c][:, :, 6], half[:, :], ALU.pow
                                ).then_inc(sig[stage, "pool"][c], 1)

            def gate(c, j):
                return gg[c][:, :, j:j + 1].to_broadcast([P, GB, P])

            def front(j, c, inst, before):
                done = sig["front", "pool"][c]
                if j == 0:
                    norm_scale("front", mv, rs, c, inst, "0")
                if j == 4:
                    wait(pool, "front", "dve", c, "g", inst)
                    g.tensor_tensor(e0[c][:, :, :], over_b(eb[:, :]), gate(c, 0), ALU.mult).then_inc(done, 1)
                    g.tensor_tensor(e1[c][:, :, :], over_b(oeb[:, :]), gate(c, 1), ALU.mult).then_inc(done, 1)
                    wait(pool, "front", "pool", c, "e1", inst)
                    g.tensor_tensor(e0[c][:, :, :], e0[c][:, :, :], e1[c][:, :, :], ALU.add).then_inc(done, 1)
                if j == 5:
                    wait(pool, "front", "pool", c, "e01", inst)
                    wait(pool, "front", "act", c, "e2", inst)
                    g.tensor_tensor(e0[c][:, :, :], e0[c][:, :, :], e2[c][:, :, :], ALU.add).then_inc(done, 1)
                if j == 6:
                    norm_scale("front", mv, rs, c, inst, "1")
                    g.tensor_tensor(x1b[c][:, :, :], x1[c][:, :, :], over_b(rows_bc[:, 0, :]), ALU.add
                                    ).then_inc(done, 1)
                if j == 10:
                    norm_scale("front", mv, rs, c, inst, "2")

            def lstm(j, c, inst, before):
                if j == 3:
                    wait(pool, "front", "dve", c, "x2", inst)
                    wait(pool, "att", "dve", c, "x3", inst - 1)
                    g.tensor_tensor(x2h[c][:, :, :], x2[c][:, :, :], ones[:, 0:1].rearrange("p (o d) -> p o d", o=1)
                                    .to_broadcast([P, GB, P]), ALU.mult).then_inc(sig["lstm", "pool"][c], 1)

            def att(j, c, inst, before):
                if j == 0:
                    norm_scale("att", amv, ars, c, inst, "")

            run(pool, "pool", {"front": front, "lstm": lstm, "att": att})

        @block.vector
        def _(dve):
            v = nc.vector
            count = [0]

            def link(ins):
                count[0] += 1
                ins.then_inc(dve_const, 1)
                dve.wait_ge(dve_const, count[0])

            dve.wait_ge(const_loaded, 16 * N_CONST)
            dve.wait_ge(pool_const, N_POOL_CONST)
            link(v.memset(half[:, :], -0.5))
            link(v.tensor_copy(rest[0:1, 0, :], bg0_row[0:1, :]))
            dve.wait_ge(pe_const, 1)
            link(v.tensor_copy(rest[0:1, 1, :], bank[0][0:1, 0:P]))
            for term in range(3):
                link(v.tensor_copy(part[0:1, :, term, :], rest[0:1, :, :]))
                if term < 2:
                    link(v.tensor_tensor(rest[0:1, :, :], rest[0:1, :, :], part[0:1, :, term, :], ALU.subtract))
            for i in range(3):
                link(v.tensor_copy(pairs_row[0:1, 0, 3 * i:3 * i + 3, :],
                                   part[0:1, 0, i:i + 1, :].to_broadcast([1, 3, P])))
            for i in range(3):
                link(v.tensor_copy(pairs_row[0:1, 1, 3 * i:3 * i + 3, :], part[0:1, 1, :, :]))
            link(v.tensor_copy(identb[:, :], ident[:, :]))
            dve.sem_inc(pairs_ready, 1)
            for src, dst in ((adjT, a_in), (adj_n, a_out)):
                link(v.tensor_scalar(scr[:, :], src[:, :], 0.0, None, ALU.is_gt))
                link(v.scalar_tensor_tensor(out=org[:, :], in0=src[:, :], scalar=0.0, in1=scr[:, :],
                                            op0=ALU.min, op1=ALU.add))
                link(v.tensor_tensor(dst[:, :], org[:, :], adjT[:, :], ALU.mult))
            link(v.tensor_scalar(maskb[:, :], adj_n[:, :], 0.0, MASKED, ALU.is_equal, ALU.mult))
            link(v.tensor_tensor(gb[:, :, :], lb[:, 0, :, :], lb[:, 1, :, :], ALU.add))
            link(v.tensor_scalar(gb[:, :, I:G], gb[:, :, I:G], 0.5, None, ALU.mult))
            link(v.tensor_scalar(gb[:, :, O:O + 1], gb[:, :, O:O + 1], 0.5, None, ALU.mult))
            link(v.tensor_scalar(WihT[:, 1:, :], WihT[:, 1:, :], 0.5, None, ALU.mult))
            link(v.tensor_scalar(WhhT[:, :, :], WhhT[:, :, :], 0.5, None, ALU.mult))
            dve.wait_ge(pe_const, 2)
            link(v.tensor_copy(rows_bc[:, :, :], bank[1][:, :].rearrange("p (k d) -> p k d", d=P)))
            for k, dst in ((2, attW[:, P:P + 1]), (3, wa2[:, :])):
                link(v.tensor_tensor(scr[:, :], attW[:, 0:P], rows_bc[:, k, :], ALU.mult))
                link(v.tensor_reduce(dst, scr[:, :], AX_X, ALU.add))
            link(v.tensor_scalar(wa2_bc[:, :], ones[:, :], wa2[:, 0:1], None, ALU.mult))
            dve.sem_inc(consts_ready, 1)

            def norm_stats(stage, src, st_t, mv_t, c, inst, tag):
                done = sig[stage, "dve"][c]
                for b in range(GB):
                    ins = v.bn_stats(st_t[c][:, b, :], src[c][:, b, :])
                ins.then_inc(done, 1)
                even, odd = st_t[c][:, :, 1:3], st_t[c][:, :, 4:6]
                wait(dve, stage, "dve", c, "st" + tag, inst)
                v.tensor_tensor(mv_t[c][:, :, 0:2], even, odd, ALU.add).then_inc(done, 1)
                v.tensor_tensor(mv_t[c][:, :, 2], even[:, :, 0], odd[:, :, 0], ALU.subtract).then_inc(done, 1)
                wait(dve, stage, "dve", c, "d" + tag, inst)
                v.scalar_tensor_tensor(out=mv_t[c][:, :, 3], in0=mv_t[c][:, :, 2], scalar=P / 4.0,
                                       in1=mv_t[c][:, :, 2], op0=ALU.mult, op1=ALU.mult).then_inc(done, 1)
                wait(dve, stage, "dve", c, "dd" + tag, inst)
                v.tensor_tensor(mv_t[c][:, :, 4], mv_t[c][:, :, 1], mv_t[c][:, :, 3], ALU.add).then_inc(done, 1)
                wait(dve, stage, "dve", c, "m2" + tag, inst)
                v.tensor_scalar(mv_t[c][:, :, 5], mv_t[c][:, :, 0], 0.5, None, ALU.mult)
                v.tensor_scalar(mv_t[c][:, :, 6], mv_t[c][:, :, 4], 1.0 / P, EPS, ALU.mult, ALU.add).then_inc(done, 1)

            def normed(stage, dst, src, mv_t, rs_t, c, inst, tag):
                wait(dve, stage, "pool", c, "rs" + tag, inst)
                for b in range(GB):
                    ins = v.tensor_scalar(dst[c][:, b, :], src[c][:, b, :], mv_t[c][:, b, 5:6], rs_t[c][:, b:b + 1],
                                          ALU.subtract, ALU.mult)
                ins.then_inc(sig[stage, "dve"][c], 1)

            def gate(c, j):
                return gg[c][:, :, j:j + 1].to_broadcast([P, GB, P])

            def front(j, c, inst, before):
                done = sig["front", "dve"][c]
                if j == 0:
                    dve.wait_ge(x_loaded[c], 16 * (inst + 1))
                    norm_stats("front", xin, st, mv, c, inst, "0")
                if j == 1:
                    normed("front", xn, xin, mv, rs, c, inst, "0")
                if j == 3:
                    wait(dve, "front", "pe", c, "gates", inst)
                    v.tensor_tensor(gz[c][:, :, :], Rb[c][:, 0:3 * GB].rearrange("p (b k) -> p b k", k=3),
                                    gbias[:, :].rearrange("p (o k) -> p o k", o=1).to_broadcast([P, GB, 3]),
                                    ALU.add).then_inc(done, 1)
                if j == 4:
                    wait(dve, "front", "act", c, "tanh", inst)
                    v.tensor_scalar(gg[c][:, :, :], gt[c][:, :, :], 0.5, 0.5, ALU.mult, ALU.add).then_inc(done, 1)
                if j == 5:
                    wait(dve, "front", "dve", c, "g", inst)
                    wait(dve, "front", "pe", c, "in", inst)
                    v.tensor_tensor(u1[c][:, :, :], as_b(Ra[c]), gate(c, 0), ALU.mult).then_inc(done, 1)
                    wait(dve, "front", "pe", c, "out", inst)
                    v.tensor_tensor(u2[c][:, :, :], as_b(Rb[c]), gate(c, 1), ALU.mult).then_inc(done, 1)
                    wait(dve, "front", "dve", c, "u2", inst)
                    v.tensor_tensor(flat(u1[c]), flat(u1[c]), flat(u2[c]), ALU.add).then_inc(done, 1)
                if j == 6:
                    wait(dve, "front", "dve", c, "u", inst)
                    wait(dve, "front", "pool", c, "e", inst)
                    v.tensor_tensor(flat(u1[c]), flat(u1[c]), flat(e0[c]), ALU.add).then_inc(done, 1)
                    wait(dve, "front", "dve", c, "s", inst)
                    v.scalar_tensor_tensor(out=flat(x1[c]), in0=flat(u1[c]), scalar=0.0, in1=flat(xin[c]),
                                           op0=ALU.max, op1=ALU.add).then_inc(done, 1)
                    wait(dve, "front", "dve", c, "x1", inst)
                    norm_stats("front", x1, st, mv, c, inst, "1")
                if j == 7:
                    normed("front", xn, x1, mv, rs, c, inst, "1")
                if j in (8, 9):
                    b = 2 * (j - 8) + 1
                    wait(dve, "front", "pe", c, f"z{b}", inst)
                    v.tensor_copy(z[c][:, b, :, :], Rb[c][:, 0:3 * P].rearrange("p (k n) -> p k n", k=3)
                                  ).then_inc(done, 1)
                if j == 10:
                    wait(dve, "front", "pe", c, "sem", inst)
                    wait(dve, "front", "pool", c, "x1b", inst)
                    wait(dve, "lstm", "pool", c, "hold", inst - 1)
                    v.tensor_tensor(flat(x2[c]), Ra[c][:, :], flat(x1b[c]), ALU.add).then_inc(done, 1)
                    wait(dve, "front", "dve", c, "x2", inst)
                    norm_stats("front", x2, st, mv, c, inst, "2")
                if j == 11:
                    normed("front", xn, x2, mv, rs, c, inst, "2")
                if j == 12:
                    wait(dve, "front", "pe", c, "q", inst)
                    v.tensor_copy(flat(q[c]), Rb[c][:, :]).then_inc(done, 1)
                if j == 14:
                    wait(dve, "front", "pe", c, "w1", inst)
                    v.tensor_tensor(y1[c][:, :, :], as_b(Rb[c]), over_b(rows_bc[:, 1, :]), ALU.add
                                    ).then_inc(done, 1)

            def lstm(j, c, inst, before):
                done = sig["lstm", "dve"][c]
                p, s = LSTM_STEPS[j // 2]
                at, n = f"{p}.{s}", GB * (P // p)
                if j % 2 == 0:
                    wait(dve, "lstm", "act", c, at + "g", inst)
                    v.scalar_tensor_tensor(out=(ig if s else c2)[c][:, 0:n], in0=ti[c][:, 0:n], scalar=1.0,
                                           in1=tg[c][:, 0:n], op0=ALU.add, op1=ALU.mult).then_inc(done, 1)
                    if s:
                        wait(dve, "lstm", "act", c, at + "f", inst)
                        v.scalar_tensor_tensor(out=fc[c][:, 0:n], in0=tf[c][:, 0:n], scalar=1.0,
                                               in1=c2[c][:, 0:n], op0=ALU.add, op1=ALU.mult).then_inc(done, 1)
                        wait(dve, "lstm", "dve", c, at + "fc", inst)
                        v.scalar_tensor_tensor(out=c2[c][:, 0:n], in0=fc[c][:, 0:n], scalar=0.5,
                                               in1=ig[c][:, 0:n], op0=ALU.mult, op1=ALU.add).then_inc(done, 1)
                else:
                    wait(dve, "lstm", "act", c, at + "tc", inst)
                    if p == 1:
                        wait(dve, "att", "pe", c, "h", inst - 1)
                    a, b = to[c][:, 0:n], tc[c][:, 0:n]
                    if s < p - 1:
                        dst = hs[c][:, 0:n]
                    else:
                        dst = H[c][:, :, s:s + (P // p - 1) * p + 1:p]
                        a, b = (t.rearrange("p (b w) -> p b w", b=GB) for t in (a, b))
                    v.scalar_tensor_tensor(out=dst, in0=a, scalar=1.0, in1=b, op0=ALU.add, op1=ALU.mult
                                           ).then_inc(done, 1)

            def att(j, c, inst, before):
                done = sig["att", "dve"][c]
                if j == 0:
                    wait(dve, "att", "pe", c, "h", inst)
                    wait(dve, "lstm", "pool", c, "hold", inst)
                    v.scalar_tensor_tensor(out=flat(x3[c]), in0=Ra[c][:, :], scalar=0.5, in1=flat(x2h[c]),
                                           op0=ALU.mult, op1=ALU.add).then_inc(done, 1)
                    wait(dve, "att", "dve", c, "x3", inst)
                    norm_stats("att", x3, ast, amv, c, inst, "")
                if j == 1:
                    normed("att", axn, x3, amv, ars, c, inst, "")
                if j == 3:
                    wait(dve, "att", "pe", c, "wh23", inst)
                    v.tensor_copy(wh[c][:, 2:4, 0:P + 1], Rb[c][:, 0:2 * (P + 1)].rearrange("p (b k) -> p b k", b=2)
                                  ).then_inc(done, 1)
                if j == 4:
                    wait(dve, "att", "act", c, "wh", inst)
                    wait(dve, "att", "dve", c, "wh", inst)
                    wait(dve, "att", "pe", c, "z", inst)
                    v.tensor_tensor(ee[c][:, :, :], as_b(Ra[c]), wh[c][:, :, P:P + 1].to_broadcast([P, GB, P]),
                                    ALU.add).then_inc(done, 1)
                    wait(dve, "att", "dve", c, "ee", inst)
                    v.scalar_tensor_tensor(out=flat(pr[c]), in0=flat(ee[c]), scalar=ALPHA, in1=flat(ee[c]),
                                           op0=ALU.mult, op1=ALU.max).then_inc(done, 1)
                    v.tensor_reduce(n0[c][:, :], ee[c][:, :, :], AX_X, ALU.max, negate=True).then_inc(done, 1)
                    wait(dve, "att", "dve", c, "n0", inst)
                    v.scalar_tensor_tensor(out=nm[c][:, :], in0=n0[c][:, :], scalar=ALPHA, in1=n0[c][:, :],
                                           op0=ALU.mult, op1=ALU.min).then_inc(done, 1)
                if j == 7:
                    for half_no, R in ((0, Ra), (1, Rb)):
                        wait(dve, "att", "pe", c, ("num01", "num23")[half_no], inst)
                        v.reciprocal(rc[c][:, 2 * half_no:2 * half_no + 2, :],
                                     R[c][:, 0:2 * (P + 2)].rearrange("p (b k) -> p b k", b=2)[:, :, P + 1:P + 2]
                                     ).then_inc(done, 1)
                    wait(dve, "att", "dve", c, "r23", inst)
                    dve.wait_ge(out_free[c], 16 * (inst + 1))
                    for b in range(GB):
                        R = (Ra, Rb)[b // 2][c][:, b % 2 * (P + 2):b % 2 * (P + 2) + P]
                        ins = v.scalar_tensor_tensor(out=xo[c][:, b, :], in0=R, scalar=rc[c][:, b, 0:1],
                                                     in1=x3[c][:, b, :], op0=ALU.mult, op1=ALU.add)
                    ins.then_inc(done, 1)

            run(dve, "dve", {"front": front, "lstm": lstm, "att": att})

        @block.scalar
        def _(act):
            a = nc.scalar.activation
            act.wait_ge(consts_ready, 1)

            def front(j, c, inst, before):
                done = sig["front", "act"][c]
                if j in (1, 7, 11):
                    tag = {1: "0", 7: "1", 11: "2"}[j]
                    wait(act, "front", "dve", c, "xn" + tag, inst)
                    a(flat(h[c]), flat(xn[c]), ACT.Relu).then_inc(done, 1)
                if j == 2:
                    wait(act, "front", "pe", c, "hT", inst)
                    a(flat(hT[c]), Ra[c][:, :], ACT.Copy).then_inc(done, 1)
                if j == 3:
                    wait(act, "front", "dve", c, "gz", inst)
                    a(gt[c][:, :, :], gz[c][:, :, :], ACT.Tanh, scale=0.5).then_inc(done, 1)
                if j == 4:
                    wait(act, "front", "dve", c, "g", inst)
                    for b in range(GB):
                        ins = a(e2[c][:, b, :], h[c][:, b, :], ACT.Copy, scale=gg[c][:, b, 2:3])
                    ins.then_inc(done, 1)
                if j in (8, 9):
                    b = 2 * (j - 8)
                    wait(act, "front", "pe", c, f"z{b}", inst)
                    a(z[c][:, b, :, :], Ra[c][:, 0:3 * P].rearrange("p (k n) -> p k n", k=3), ACT.Copy
                      ).then_inc(done, 1)
                if j == 13:
                    wait(act, "front", "pe", c, "w0", inst)
                    a(flat(y0[c]), Ra[c][:, :], ACT.Relu).then_inc(done, 1)
                if j == 15:
                    wait(act, "front", "pe", c, "w2", inst)
                    wait(act, "lstm", "pe", c, "1.0o", inst - 1)
                    a(flat(hin[c]), Ra[c][:, :], ACT.Relu).then_inc(done, 1)

            def lstm(j, c, inst, before):
                done = sig["lstm", "act"][c]
                p, s = LSTM_STEPS[j // 2]
                at, n = f"{p}.{s}", GB * (P // p)

                def gate(dst, src, which):
                    a(dst[c][:, 0:n], src, ACT.Tanh, bias=gb[:, p - 1, which:which + 1],
                      scale=1.0 if which == G else 0.5).then_inc(done, 1)

                if p == 1:
                    if j % 2 == 0:
                        wait(act, "lstm", "dve", c, "4.3h", inst - 1)
                        wait(act, "lstm", "pe", c, at + "i", inst)
                        gate(ti, La[c][:, :], I)
                        wait(act, "lstm", "pe", c, at + "g", inst)
                        gate(tg, Lb[c][:, :], G)
                    else:
                        wait(act, "lstm", "pe", c, at + "o", inst)
                        gate(to, La[c][:, :], O)
                elif j % 2 == 0:
                    wait(act, "lstm", "pe", c, at + "ig", inst)
                    gate(ti, La[c][:, 0:n], I)
                    gate(tg, La[c][:, COLS // 2:COLS // 2 + n], G)
                    wait(act, "lstm", "pe", c, at + "fo", inst)
                    if s:
                        gate(tf, Lb[c][:, 0:n], F)
                    gate(to, Lb[c][:, COLS // 2:COLS // 2 + n], O)
                if j % 2:
                    wait(act, "lstm", "dve", c, at + "c", inst)
                    a(tc[c][:, 0:n], c2[c][:, 0:n], ACT.Tanh, scale=0.5).then_inc(done, 1)

            def att(j, c, inst, before):
                done = sig["att", "act"][c]
                if j == 1:
                    wait(act, "att", "dve", c, "xn", inst)
                    a(flat(ah[c]), flat(axn[c]), ACT.Relu).then_inc(done, 1)
                if j == 2:
                    wait(act, "att", "pe", c, "hT", inst)
                    a(flat(ahT[c]), Rb[c][:, :], ACT.Copy).then_inc(done, 1)
                if j == 3:
                    wait(act, "att", "pe", c, "wh01", inst)
                    a(wh[c][:, 0:2, 0:P + 1], Ra[c][:, 0:2 * (P + 1)].rearrange("p (b k) -> p b k", b=2), ACT.Copy
                      ).then_inc(done, 1)
                if j == 5:
                    wait(act, "att", "dve", c, "nm", inst)
                    for b in range(GB):
                        ins = a(ee[c][:, b, :], pr[c][:, b, :], ACT.Exp, bias=nm[c][:, b:b + 1])
                    ins.then_inc(done, 1)
                if j == 6:
                    wait(act, "att", "pe", c, "aT", inst)
                    a(flat(aT[c]), Rb[c][:, :], ACT.Copy).then_inc(done, 1)

            run(act, "act", {"front": front, "lstm": lstm, "att": att})

        @block.tensor
        def _(pe):
            mm_ = nc.tensor.matmul
            pe.wait_ge(const_loaded, 16 * N_CONST)
            pe.wait_ge(pool_const, N_POOL_CONST)
            mm_(bank[0][0:1, 0:P], ones[:, 0:1], adjT[:, :], start=True, stop=True).then_inc(pe_const, 1)
            mm_(bank[1][:, :], ones[0:1, :], rows_t[0:1, :, :].rearrange("p k d -> p (k d)"), start=True, stop=True
                ).then_inc(pe_const, 1)
            pe.wait_ge(consts_ready, 1)
            pe.wait_ge(pairs_moved, 32)

            def bank_free(c, which, before):
                if before is not None:
                    stage, inst = before
                    who, step = {("front", "a"): ("act", "hin"), ("front", "b"): ("dve", "y1"),
                                 ("att", "a"): ("dve", "out"), ("att", "b"): ("dve", "out")}[stage, which]
                    wait(pe, stage, who, c, step, inst)

            def front(j, c, inst, before):
                done = sig["front", "pe"][c]
                if j == 2:
                    wait(pe, "front", "act", c, "h0", inst)
                    bank_free(c, "a", before)
                    for b in range(GB):
                        ins = nc.tensor.transpose(Ra[c][:, b * P:(b + 1) * P], h[c][:, b, :], ident[:, :])
                    ins.then_inc(done, 1)
                if j == 3:
                    wait(pe, "front", "act", c, "hT", inst)
                    bank_free(c, "b", before)
                    for b in range(GB):
                        ins = mm_(Rb[c][:, 3 * b:3 * b + 3], hT[c][:, b, :], gvec[:, :], start=True, stop=True)
                    ins.then_inc(done, 1)
                if j == 4:
                    mm_(Ra[c][:, :], a_in[:, :], flat(h[c]), start=True, stop=True).then_inc(done, 1)
                    wait(pe, "front", "dve", c, "gz", inst)
                    mm_(Rb[c][:, :], a_out[:, :], flat(h[c]), start=True, stop=True).then_inc(done, 1)
                if j in (8, 9):
                    for b, R in ((2 * (j - 8), Ra), (2 * (j - 8) + 1, Rb)):
                        if b == 0:
                            wait(pe, "front", "act", c, "h1", inst)
                        if b == 2:
                            wait(pe, "front", "act", c, "z0", inst)
                        if b == 3:
                            wait(pe, "front", "dve", c, "z1", inst)
                        mm_(R[c][:, 0:3 * P], h[c][:, b, :], a_sem[:, :, :].rearrange("p k n -> p (k n)"),
                            start=True, stop=True).then_inc(done, 1)
                if j == 10:
                    wait(pe, "front", "act", c, "z2", inst)
                    wait(pe, "front", "dve", c, "z3", inst)
                    for b in range(GB):
                        for k in range(3):
                            ins = mm_(Ra[c][:, b * P:(b + 1) * P], z[c][:, b, k, :], semW[:, k, :],
                                      start=k == 0, stop=k == 2)
                    ins.then_inc(done, 1)
                if j == 12:
                    wait(pe, "front", "act", c, "h2", inst)
                    for b in range(GB):
                        ins = mm_(Rb[c][:, b * P:(b + 1) * P], h[c][:, b, :], adjT[:, :], start=True, stop=True)
                    ins.then_inc(done, 1)
                if j == 13:
                    wait(pe, "front", "dve", c, "q", inst)
                    mm_(Ra[c][:, :], Wg[:, 0, :], flat(q[c]), start=True, stop=False)
                    mm_(as_b(Ra[c]), bg0_9[0:9, :], rs_9[0:9, :].rearrange("p (o n) -> p o n", o=1)
                        .to_broadcast([9, GB, P]), start=False, stop=True).then_inc(done, 1)
                if j == 14:
                    wait(pe, "front", "act", c, "y0", inst)
                    for b in range(GB):
                        ins = mm_(Rb[c][:, b * P:(b + 1) * P], y0[c][:, b, :], Wg[:, 1, :], start=True, stop=True)
                    ins.then_inc(done, 1)
                if j == 15:
                    wait(pe, "front", "dve", c, "y1", inst)
                    for b in range(GB):
                        ins = mm_(Ra[c][:, b * P:(b + 1) * P], y1[c][:, b, :], adjT[:, :], start=True, stop=True)
                    ins.then_inc(done, 1)

            def lstm(j, c, inst, before):
                done = sig["lstm", "pe"][c]
                p, s = LSTM_STEPS[j // 2]
                at, nw = f"{p}.{s}", P // p
                n = GB * nw
                if p == 1:
                    def product(R, which):
                        mm_(R[c][:, :], WihT[:, 0, which * P:(which + 1) * P], flat(hin[c]), start=True, stop=True
                            ).then_inc(done, 1)
                    if j % 2 == 0:
                        wait(pe, "front", "act", c, "hin", inst)
                        wait(pe, "lstm", "act", c, "4.3o", inst - 1)
                        product(La, I)
                        product(Lb, G)
                    else:
                        wait(pe, "lstm", "act", c, at + "i", inst)
                        product(La, O)
                    return

                def gates(first):
                    for which, R, col in ((I, La, 0), (G, La, COLS // 2), (F, Lb, 0), (O, Lb, COLS // 2)):
                        if not (first and which == F):
                            yield which, R[c][:, col:col + n]

                def from_x(at_s):
                    rhs = H[c][:, :, at_s:at_s + (nw - 1) * p + 1:p]
                    for which, dst in gates(at_s == 0):
                        opens = which in (I, F) or (which == O and at_s == 0)
                        ins = mm_(dst.rearrange("p (b w) -> p b w", b=GB),
                                  WihT[:, p - 1, which * P:(which + 1) * P], rhs, start=opens, stop=at_s == 0,
                                  skip_group_check=True)
                        if at_s == 0 and which in (G, O):
                            ins.then_inc(done, 1)

                if j % 2 == 0 and s == 0:
                    wait(pe, "lstm", "dve", c, f"{p - 1}.{p - 2}h", inst)
                    from_x(0)
                elif j % 2 == 0:
                    wait(pe, "lstm", "dve", c, f"{p}.{s - 1}h", inst)
                    for which, dst in gates(False):
                        ins = mm_(dst, WhhT[:, p - 2, which * P:(which + 1) * P], hs[c][:, 0:n], start=False,
                                  stop=True, skip_group_check=True)
                        if which in (G, O):
                            ins.then_inc(done, 1)
                elif s + 1 < p:
                    wait(pe, "lstm", "act", c, at + "o", inst)
                    from_x(s + 1)

            def att(j, c, inst, before):
                done = sig["att", "pe"][c]
                if j == 0:
                    wait(pe, "lstm", "dve", c, "4.3h", inst)
                    bank_free(c, "a", before)
                    for b in range(GB):
                        ins = nc.tensor.transpose(Ra[c][:, b * P:(b + 1) * P], H[c][:, b, :], ident[:, :])
                    ins.then_inc(done, 1)
                if j == 2:
                    wait(pe, "att", "act", c, "h3", inst)
                    bank_free(c, "b", before)
                    for b in range(GB):
                        ins = nc.tensor.transpose(Rb[c][:, b * P:(b + 1) * P], ah[c][:, b, :], ident[:, :])
                    ins.then_inc(done, 1)
                if j == 3:
                    wait(pe, "att", "act", c, "hT", inst)
                    for R, b0 in ((Ra, 0), (Rb, 2)):
                        for b in (0, 1):
                            ins = mm_(R[c][:, b * (P + 1):(b + 1) * (P + 1)], ahT[c][:, b0 + b, :], attW[:, 0:P + 1],
                                      start=True, stop=True)
                        ins.then_inc(done, 1)
                if j == 4:
                    wait(pe, "att", "act", c, "wh", inst)
                    mm_(Ra[c][:, :], wa2_bc[:, :], flat(ahT[c]), start=True, stop=False)
                    mm_(as_b(Ra[c]), identb[:, :], over_b(maskb[:, :]), start=False, stop=True).then_inc(done, 1)
                if j == 6:
                    wait(pe, "att", "act", c, "p", inst)
                    wait(pe, "att", "dve", c, "wh", inst)
                    for b in range(GB):
                        ins = nc.tensor.transpose(Rb[c][:, b * P:(b + 1) * P], ee[c][:, b, :], ident[:, :])
                    ins.then_inc(done, 1)
                if j == 7:
                    for R, b0 in ((Ra, 0), (Rb, 2)):
                        wait(pe, "att", "act", c, "aT", inst)
                        for b in (0, 1):
                            ins = mm_(R[c][:, b * (P + 2):(b + 1) * (P + 2)], aT[c][:, b0 + b, :],
                                      wh[c][:, b0 + b, :], start=True, stop=True)
                        ins.then_inc(done, 1)

            run(pe, "pe", {"front": front, "lstm": lstm, "att": att})


def kernel(**inputs):
    import numpy as np
    import concourse.bacc as bacc
    from concourse.bass_utils import run_bass_kernel_spmd

    t = {name: np.asarray(a) for name, a in inputs.items()}
    lstm_b = [t[f"L2_gnn_{b}"].reshape(MAX_SKIP, 4, P).transpose(2, 0, 1) for b in ("bih", "bhh")]
    arrays = {
        "x": t["x"],
        "adj": t["adj"],
        "adj_t": t["adj"].T,
        "edge_bias": t["L0_gnn_edge_bias"],
        "out_edge_bias": t["L0_gnn_out_edge_bias"],
        "gate_vecs": np.concatenate([t["L0_gnn_gate_weight"], t["L0_gnn_out_gate_weight"],
                                     t["L0_gnn_loop_gate"]], axis=1),
        "gate_biases": np.concatenate([t["L0_gnn_bias_gate"], t["L0_gnn_out_bias_gate"],
                                       np.zeros((P, 1), np.float32)], axis=1),
        "sem_w": t["L1_gnn_W"],
        "rows": np.stack([t["L1_gnn_bias"], t["L2_gnn_bg1"], t["L3_gnn_a"][:P, 0], t["L3_gnn_a"][P:, 0],
                          t["L2_gnn_bg0"]]),
        "gcn_w": np.stack([t["L2_gnn_Wg0"], t["L2_gnn_Wg1"]]),
        "wih_t": t["L2_gnn_Wih"].transpose(0, 2, 1),
        "whh_t": t["L2_gnn_Whh"][1:].transpose(0, 2, 1),
        "lstm_b": np.stack(lstm_b),
        "att_w": t["L3_gnn_W"],
    }
    arrays = {f"in_{name}": np.ascontiguousarray(a) for name, a in arrays.items()}
    nc = bacc.Bacc("TRN2", target_bir_lowering=False, num_devices=1)
    aps = [nc.dram_tensor(name, a.shape, mybir.dt.from_np(a.dtype), kind="ExternalInput").ap()
           for name, a in arrays.items()]
    out = nc.dram_tensor("out", t["x"].shape, F32, kind="ExternalOutput").ap()
    graph_layers_kernel(nc, *aps, out)
    return run_bass_kernel_spmd(nc, [arrays], core_ids=[0]).results[0]["out"]
```

```python
from contextlib import ExitStack

import concourse.bass as bass
from concourse import mybir

F32 = mybir.dt.float32
F32R = mybir.dt.float32r
BF16 = mybir.dt.bfloat16
ALU = mybir.AluOpType
ACT = mybir.ActivationFunctionType
AX_X = mybir.AxisListType.X

P = 128
GB = 4
CHAINS = 2
COLS = GB * P
MAX_SKIP = 4
EPS = 1e-5
ALPHA = 0.2
MASKED = -float(2 ** 100)
I, F, G, O = range(4)

LSTM_STEPS = [(p, s) for p in range(1, MAX_SKIP + 1) for s in range(p)]


def _lstm_names():
    pe, act, dve, pool = [], [], [], []
    for p, s in LSTM_STEPS:
        at = f"{p}.{s}"
        if p == 1:
            pe += [at + "i", at + "g", at + "o"]
            act += [at + "i", at + "g", at + "o", at + "tc", at + "H"]
            pool += [at + "L"]
            dve += [at + "c", at + "h"]
        else:
            pe += [at + "ig", at + "fo"]
            act += [at + "i", at + "g"] + ([at + "f"] if s else []) + [at + "o", at + "tc"]
            dve += ([at + "ig", at + "fc"] if s else []) + [at + "c", at + "h"]
            if 1 < p < MAX_SKIP and s == p - 1:
                act += [at + "H"]
                pool += [at + "L"]
    return pe, act, dve, pool


ROUND = 10000
LAG = 5001
PLACES = {
    "pe": {
        "front": {20: -4900, 30: -4195, 40: -3948, 41: -3725, 80: -1480, 90: -1431, 91: -413, 100: -137},
        "gcn": {0: 480, 10: 820, 20: 1054, 30: 1367},
        "lstm": {0: 2016, 10: 2596, 20: 3551, 30: 4598, 40: 4598, 60: 4908, 70: 5057, 80: 5058, 90: 5461,
                 100: 5931, 120: 6838, 140: 7504, 150: 8438, 160: 8438, 180: 9845},
        "att": {0: 10168, 20: 11441, 30: 11874, 40: 13378, 60: 14892, 70: 15038, 71: 15038},
    },
    "act": {
        "front": {10: -5665, 20: -4526, 30: -3953, 40: -3478, 70: -2238, 71: -2058, 80: -1572, 90: -1230, 110: 680},
        "gcn": {0: 687, 10: 1162, 30: 1906},
        "lstm": {0: 2375, 1: 2375, 10: 2488, 11: 2488, 12: 2944, 20: 3494, 21: 3494, 30: 3738, 40: 4217, 41: 4222,
                 50: 4280, 51: 4955, 60: 5121, 61: 5121, 70: 5334, 80: 5334, 81: 5386, 90: 5729, 100: 6497,
                 101: 6501, 110: 6681, 111: 6879, 120: 6968, 121: 7021, 130: 7080, 140: 7454, 141: 7454, 150: 7792,
                 160: 8269, 161: 8269, 170: 8743, 180: 9269, 181: 9269, 190: 10225},
        "att": {10: 11597, 20: 11950, 30: 12093, 50: 14198, 60: 15030},
    },
    "dve": {
        "front": {0: -8833, 1: -8817, 2: -8695, 3: -7038, 10: -7007, 30: -3988, 40: -3853, 50: -3718, 51: -3696,
                  52: -3696, 60: -3678, 61: -3552, 62: -3506, 63: -3447, 64: -3391, 65: -3391, 70: -3335,
                  80: -2212, 90: -2050, 100: -1217, 101: -1217, 102: -1204, 103: -1186, 104: -1156, 110: -1067},
        "gcn": {20: 1286, 30: 1399},
        "lstm": {0: 1641, 10: 1670, 20: 2810, 30: 2945, 40: 3262, 41: 3262, 42: 3473, 50: 3692, 60: 3789, 70: 3831,
                 80: 3986, 81: 3986, 82: 4193, 90: 6041, 100: 6201, 101: 6201, 102: 6201, 110: 6291, 120: 6450,
                 130: 6521, 140: 6651, 141: 6651, 142: 6667, 150: 7533, 160: 7619, 161: 7777, 162: 7902, 170: 7972,
                 180: 8286, 181: 8566, 182: 8609, 190: 8879},
        "att": {0: 9170, 1: 9171, 2: 9307, 3: 9308, 4: 9308, 10: 11182, 30: 12565, 40: 12565, 41: 12565, 42: 12601,
                70: 13804, 71: 13870, 72: 13870},
    },
    "pool": {
        "front": {0: -7463, 40: -5380, 41: -5380, 50: -5380, 60: -2476, 100: -1103},
        "lstm": {10: 2530, 30: 3381, 50: 3701, 110: 4948},
        "att": {0: 9420},
    },
}
_LPE, _LACT, _LDVE, _LPOOL = _lstm_names()

STEPS = {
    "front": {
        "pe": ["hT", "gates", "in", "out", "z0", "z1", "z2", "z3", "sem"],
        "act": ["h0", "hT", "tanh", "e2", "h1", "dh", "z0", "z2", "h2"],
        "dve": ["st0", "sv0", "d0", "dd0", "mv0", "xn0", "gz", "g", "u1", "u2", "u", "s", "x1", "st1", "sv1", "d1", "dd1", "mv1", "xn1", "z1", "z3",
                "x2", "st2", "sv2", "d2", "dd2", "mv2", "xn2"],
        "pool": ["rs0", "e0", "e1", "e01", "e", "rs1", "x1b", "rs2"],
    },
    "gcn": {"pe": ["q", "w0", "w1", "w2"], "act": ["q", "y0", "hin"], "dve": ["y1", "hinL"]},
    "lstm": {"pe": _LPE, "act": _LACT, "dve": _LDVE, "pool": _LPOOL[:1] + ["hold"] + _LPOOL[1:]},
    "att": {
        "pe": ["h", "hT", "wh01", "wh23", "z", "aT", "num01", "num23"],
        "act": ["h3", "hT", "wh", "p", "aT"],
        "dve": ["x3", "st", "sv", "d", "dd", "mv", "xn", "wh", "ee", "lr", "n0", "nm", "r01", "r23", "out"],
        "pool": ["rs"],
    },
}


def graph_layers_kernel(nc, x, graph, gate_cols, rows, sem_gcn_w, wih_t, whh_t, lstm_b, att_w, out):
    B, N, D = x.shape
    assert N == P and D == P and B % (GB * CHAINS) == 0
    ROUNDS = B // (GB * CHAINS)
    assert ROUNDS >= 4

    ctx = ExitStack()
    with ctx:
        def sb(name, shape, dt=F32):
            return ctx.enter_context(nc.sbuf_tensor(name, [P] + shape, dt))

        def per_chain(name, shape, dt=F32):
            return [sb(f"{name}_{c}", shape, dt) for c in range(CHAINS)]

        def sem(name):
            return ctx.enter_context(nc.semaphore(name))

        graph_t = sb("graph_t", [4, P])
        adjT = graph_t[:, 0, :]
        adj_n = graph_t[:, 1, :]
        eb = graph_t[:, 2, :]
        oeb = graph_t[:, 3, :]
        a_in = sb("a_in", [P])
        a_out = sb("a_out", [P])
        a_sem = sb("a_sem", [2, P])
        diag = sb("diag", [1])
        org = sb("org", [P])
        gate_t = sb("gate_t", [6])
        gvec = gate_t[:, 0:3]
        gbias = gate_t[:, 3:6]
        rows_t = sb("rows_t", [5, P])
        rows_bc = sb("rows_bc", [4, P])
        mats = sb("mats", [5, P])
        semW = mats[:, 0:3, :]
        Wg = mats[:, 3:5, :]
        WihT = sb("WihT", [MAX_SKIP, 4 * P])
        WihH = sb("WihH", [3, 4 * P], F32R)
        WihL = sb("WihL", [3, 4 * P], F32R)
        WhhT = sb("WhhT", [MAX_SKIP - 1, 4 * P])
        lb = sb("lb", [2, MAX_SKIP, 4])
        gb = sb("gb", [MAX_SKIP, 4])
        attW = sb("attW", [P + 2])
        wa2 = sb("wa2", [1])
        wa2_bc = sb("wa2_bc", [P])
        scr = sb("scr", [P])
        ident = sb("ident", [P])
        identb = sb("identb", [P], BF16)
        ones = sb("ones", [P])
        zero = sb("zero", [P])
        maskb = sb("maskb", [P], BF16)
        half = sb("half", [GB])
        rsum = sb("rsum", [P])
        part = sb("part", [2, 3, P], BF16)
        rest = sb("rest", [2, P])
        pairs_row = sb("pairs_row", [2, 9, P], BF16)
        bg0_9 = sb("bg0_9", [P], BF16)
        rs_9 = sb("rs_9", [P], BF16)

        xin = per_chain("xin", [GB, P])
        st = per_chain("st", [GB, 6])
        mv = per_chain("mv", [GB, 7])
        rs = per_chain("rs", [GB])
        xn = per_chain("xn", [GB, P])
        h = per_chain("h", [GB, P])
        hT = per_chain("hT", [GB, P])
        gz = per_chain("gz", [GB, 3])
        gt = per_chain("gt", [GB, 3])
        gg = per_chain("gg", [GB, 3])
        e0 = per_chain("e0", [GB, P])
        e1 = per_chain("e1", [GB, P])
        e2 = per_chain("e2", [GB, P])
        u1 = per_chain("u1", [GB, P])
        u2 = per_chain("u2", [GB, P])
        x1 = per_chain("x1", [GB, P])
        x1b = e0
        dh = e2
        z = per_chain("z", [GB, 3, P])
        x2 = per_chain("x2", [GB, P])
        x2h = per_chain("x2h", [GB, P])
        hinH = per_chain("hinH", [GB, P], F32R)
        hinL = per_chain("hinL", [GB, P], F32R)
        ti = per_chain("ti", [COLS])
        tg = per_chain("tg", [COLS])
        tf = per_chain("tf", [COLS // 2])
        to = per_chain("to", [COLS])
        c2 = per_chain("c2", [COLS])
        ig = per_chain("ig", [COLS // 2])
        fc = per_chain("fc", [COLS // 2])
        tc = per_chain("tc", [COLS])
        q, y0, y1 = ([t[c][:, :].rearrange("p (b n) -> p b n", b=GB) for c in range(CHAINS)] for t in (ti, tg, tc))
        hs = per_chain("hs", [COLS // 2])
        H = per_chain("H", [GB, P])
        HH = per_chain("HH", [GB, P], F32R)
        HL = per_chain("HL", [GB, P], F32R)
        x3 = per_chain("x3", [GB, P])
        ast = per_chain("ast", [GB, 6])
        amv = per_chain("amv", [GB, 7])
        ars = per_chain("ars", [GB])
        axn = per_chain("axn", [GB, P])
        ah = per_chain("ah", [GB, P])
        ahT = per_chain("ahT", [GB, P])
        wh = per_chain("wh", [GB, P + 2])
        n0 = per_chain("n0", [GB])
        nm = per_chain("nm", [GB])
        ee = per_chain("ee", [GB, P])
        pr = per_chain("pr", [GB, P])
        aT = per_chain("aT", [GB, P])
        rc = per_chain("rc", [GB, 1])
        xo = per_chain("xo", [GB, P])

        bank = [ctx.enter_context(nc.psum_tensor(f"bank{i}", [P, COLS], F32)) for i in range(8)]
        La, Lb = [bank[0], bank[2]], [bank[1], bank[3]]
        Ra, Rb = [bank[4], bank[6]], [bank[5], bank[7]]

        sig = {(stage, eng): [sem(f"{stage}_{eng}_{c}") for c in range(CHAINS)]
               for stage in STEPS for eng in STEPS[stage]}
        x_loaded = [sem(f"x_loaded_{c}") for c in range(CHAINS)]
        out_free = [sem(f"out_free_{c}") for c in range(CHAINS)]
        graph_loaded = sem("graph_loaded")
        weights_loaded = sem("weights_loaded")
        pool_const = sem("pool_const")
        dve_const = sem("dve_const")
        pe_const = sem("pe_const")
        pairs_ready = sem("pairs_ready")
        pairs_moved = sem("pairs_moved")
        graph_ready = sem("graph_ready")
        weights_scaled = sem("weights_scaled")
        weights_split = sem("weights_split")
        consts_ready = sem("consts_ready")

        def wait(eng, stage, who, c, step, inst):
            steps = STEPS[stage][who]
            value = inst * len(steps) + (steps.index(step) + 1)
            if not (isinstance(value, int) and value <= 0):
                eng.wait_ge(sig[stage, who][c], value)

        def over_b(t):
            return t.rearrange("p (o d) -> p o d", o=1).to_broadcast([P, GB, P])

        def flat(t):
            return t[:, :, :].rearrange("p b d -> p (b d)")

        def as_b(t):
            return t[:, :].rearrange("p (b d) -> p b d", d=P)

        N_GRAPH, N_WEIGHTS = 3, 5
        N_POOL_CONST = 5 + CHAINS
        block = ctx.enter_context(nc.Block())

        LAST = ROUNDS - 1

        def run(eng, name, parts, late_from=None, late=None):
            def part(stage, j, c, inst):
                inner = not isinstance(inst, int)
                if (stage, j, c) == ("front", late_from, 0) and not inner and inst == 0:
                    late()
                before = {"att": ("front", inst + 1) if inner or inst + 1 < ROUNDS else ("att", inst - 1),
                          "front": ("att", inst - 2) if inner or inst >= 2 else ("front", 0) if inst == 1 else None,
                          "gcn": None, "lstm": None}[stage]
                parts[stage](j // 10, j % 10, c, inst, before)

            order = []
            for stage, places in PLACES[name].items():
                for j, place in places.items():
                    for c in range(CHAINS):
                        at = place + c * LAG
                        order.append((at % ROUND, at // ROUND, stage, j, c))
            order.sort()
            begin, tail = min(o[1] for o in order), max(o[1] for o in order)

            def a_round(r):
                for _, behind, stage, j, c in order:
                    if not isinstance(r, int) or 0 <= r - behind < ROUNDS:
                        part(stage, j, c, r - behind)

            first, end = tail + 2, ROUNDS - 1 + begin
            for r in range(begin, first):
                a_round(r)
            with eng.Fori(first, end) as r:
                a_round(r)
            for r in range(end, ROUNDS + tail):
                a_round(r)

        @block.sync
        def _(sp):
            def load(c, inst):
                wait(sp, "front", "dve", c, "x1", inst - 1)
                first = (inst * CHAINS + c) * GB
                sp.dma_start(xin[c][:, :, :], x[bass.ds(first, GB), :, :].rearrange("b n d -> n b d")
                             ).then_inc(x_loaded[c], 16)

            def store(c, inst):
                wait(sp, "att", "dve", c, "out", inst)
                first = (inst * CHAINS + c) * GB
                sp.dma_start(out[bass.ds(first, GB), :, :].rearrange("b n d -> n b d"), xo[c][:, :, :]
                             ).then_inc(out_free[c], 16)

            for c in range(CHAINS):
                sp.sem_inc(out_free[c], 16)
            load(0, 0)
            for dst, src in (
                (gate_t[:, :], gate_cols),
                (graph_t[:, :, :], graph.rearrange("k i j -> i k j")),
                (rows_t[0:1, :, :], rows),
            ):
                sp.dma_start(dst, src).then_inc(graph_loaded, 16)
            load(1, 0)
            sp.wait_ge(pairs_ready, 1)
            sp.dma_start(bg0_9[0:9, :], pairs_row[0:1, 0, :, :]).then_inc(pairs_moved, 16)
            sp.dma_start(rs_9[0:9, :], pairs_row[0:1, 1, :, :]).then_inc(pairs_moved, 16)

            for c in range(CHAINS):
                load(c, 1)
            with sp.Fori(1, ROUNDS - 1) as k:
                for c in range(CHAINS):
                    load(c, k + 1)
                for c in range(CHAINS):
                    store(c, k - 1)
            for inst in (ROUNDS - 2, ROUNDS - 1):
                for c in range(CHAINS):
                    store(c, inst)
            for c in range(CHAINS):
                sp.wait_ge(out_free[c], 16 * (ROUNDS + 1))

        @block.gpsimd
        def _(pool):
            g = nc.gpsimd
            g.memset(zero[:, :], 0.0).then_inc(pool_const, 1)
            g.memset(ones[:, :], 1.0).then_inc(pool_const, 1)
            for c in range(CHAINS):
                g.memset(wh[c][:, :, P + 1:P + 2], 1.0).then_inc(pool_const, 1)
            pool.wait_ge(pool_const, 2 + CHAINS)
            g.affine_select(out=ident[:, :], in_=zero[:, :], compare_op=ALU.not_equal, fill=1.0, base=0,
                            pattern=[[-1, P]], channel_multiplier=1).then_inc(pool_const, 1)
            pool.wait_ge(graph_loaded, 16 * N_GRAPH)
            for k, sign in enumerate((1, -1)):
                g.affine_select(out=a_sem[:, k, :], in_=adjT, compare_op=ALU.is_gt, fill=0.0, base=0,
                                pattern=[[-sign, P]], channel_multiplier=sign).then_inc(pool_const, 1)
            pool.wait_ge(graph_ready, 1)

            def late_constants():
                for k, p in enumerate((1, 2, 4)):
                    pool.wait_ge(weights_scaled, k + 3)
                    g.tensor_tensor(WihL[:, k, :], WihT[:, p - 1, :], WihH[:, k, :], ALU.subtract
                                    ).then_inc(weights_split, 1)


            def norm_scale(stage, mv_t, rs_t, c, inst, tag):
                wait(pool, stage, "dve", c, "mv" + tag, inst)
                g.tensor_tensor(rs_t[c][:, :], mv_t[c][:, :, 6], half[:, :], ALU.pow
                                ).then_inc(sig[stage, "pool"][c], 1)

            def gate(c, j):
                return gg[c][:, :, j:j + 1].to_broadcast([P, GB, P])

            def front(j, k, c, inst, before):
                done = sig["front", "pool"][c]
                if j == 0:
                    norm_scale("front", mv, rs, c, inst, "0")
                if j == 4 and k == 0:
                    wait(pool, "front", "dve", c, "g", inst)
                    g.tensor_tensor(e0[c][:, :, :], over_b(eb), gate(c, 0), ALU.mult).then_inc(done, 1)
                    g.tensor_tensor(e1[c][:, :, :], over_b(oeb), gate(c, 1), ALU.mult).then_inc(done, 1)
                if j == 4 and k == 1:
                    wait(pool, "front", "pool", c, "e1", inst)
                    g.tensor_tensor(e0[c][:, :, :], e0[c][:, :, :], e1[c][:, :, :], ALU.add).then_inc(done, 1)
                if j == 5:
                    wait(pool, "front", "pool", c, "e01", inst)
                    wait(pool, "front", "act", c, "e2", inst)
                    g.tensor_tensor(e0[c][:, :, :], e0[c][:, :, :], e2[c][:, :, :], ALU.add).then_inc(done, 1)
                if j == 6:
                    norm_scale("front", mv, rs, c, inst, "1")
                    g.tensor_tensor(x1b[c][:, :, :], x1[c][:, :, :], over_b(rows_bc[:, 0, :]), ALU.add
                                    ).then_inc(done, 1)
                if j == 10:
                    norm_scale("front", mv, rs, c, inst, "2")

            def lstm(j, k, c, inst, before):
                p, s = LSTM_STEPS[j // 2]
                if j % 2 and s == p - 1 < MAX_SKIP - 1:
                    last = slice(s, s + (P // p - 1) * p + 1, p)
                    wait(pool, "lstm", "act", c, f"{p}.{s}H", inst)
                    g.tensor_tensor(HL[c][:, :, last], H[c][:, :, last], HH[c][:, :, last], ALU.subtract
                                    ).then_inc(sig["lstm", "pool"][c], 1)
                if j == 3:
                    wait(pool, "front", "dve", c, "x2", inst)
                    wait(pool, "att", "dve", c, "x3", inst - 1)
                    g.tensor_tensor(x2h[c][:, :, :], x2[c][:, :, :], ones[:, 0:1].rearrange("p (o d) -> p o d", o=1)
                                    .to_broadcast([P, GB, P]), ALU.mult).then_inc(sig["lstm", "pool"][c], 1)

            def att(j, k, c, inst, before):
                if j == 0:
                    norm_scale("att", amv, ars, c, inst, "")

            run(pool, "pool", {"front": front, "lstm": lstm, "att": att}, late_from=40, late=late_constants)

        @block.vector
        def _(dve):
            v = nc.vector
            count = [0]

            def link(ins):
                count[0] += 1
                ins.then_inc(dve_const, 1)
                dve.wait_ge(dve_const, count[0])

            link(v.memset(half[:, :], -0.5))
            dve.wait_ge(graph_loaded, 16 * N_GRAPH)
            for src, dst in ((adjT, a_in), (adj_n, a_out)):
                link(v.tensor_scalar(scr[:, :], src[:, :], 0.0, None, ALU.is_gt))
                link(v.scalar_tensor_tensor(out=org[:, :], in0=src[:, :], scalar=0.0, in1=scr[:, :],
                                            op0=ALU.min, op1=ALU.add))
                link(v.tensor_tensor(dst[:, :], org[:, :], adjT, ALU.mult))
            dve.wait_ge(pool_const, N_POOL_CONST)
            link(v.tensor_tensor(scr[:, :], adj_n, ident[:, :], ALU.mult))
            link(v.tensor_reduce(diag[:, :], scr[:, :], AX_X, ALU.add))
            dve.wait_ge(pe_const, 2)
            link(v.tensor_copy(rows_bc[:, :, :], bank[1][:, :].rearrange("p (k d) -> p k d", d=P)))
            dve.sem_inc(graph_ready, 1)

            def late_constants():
                link(v.tensor_copy(rest[0:1, 0, :], rows_t[0:1, 4, :]))
                link(v.tensor_copy(rest[0:1, 1, :], bank[0][0:1, 0:P]))
                for term in range(3):
                    link(v.tensor_copy(part[0:1, :, term, :], rest[0:1, :, :]))
                    if term < 2:
                        link(v.tensor_tensor(rest[0:1, :, :], rest[0:1, :, :], part[0:1, :, term, :], ALU.subtract))
                for i in range(3):
                    link(v.tensor_copy(pairs_row[0:1, 0, 3 * i:3 * i + 3, :],
                                       part[0:1, 0, i:i + 1, :].to_broadcast([1, 3, P])))
                for i in range(3):
                    link(v.tensor_copy(pairs_row[0:1, 1, 3 * i:3 * i + 3, :], part[0:1, 1, :, :]))
                dve.sem_inc(pairs_ready, 1)
                link(v.tensor_copy(identb[:, :], ident[:, :]))
                link(v.tensor_scalar(maskb[:, :], adj_n, 0.0, MASKED, ALU.is_equal, ALU.mult))
                dve.wait_ge(weights_loaded, 16 * N_WEIGHTS)
                link(v.tensor_tensor(gb[:, :, :], lb[:, 0, :, :], lb[:, 1, :, :], ALU.add))
                link(v.tensor_scalar(gb[:, :, I:G], gb[:, :, I:G], 0.5, None, ALU.mult))
                link(v.tensor_scalar(gb[:, :, O:O + 1], gb[:, :, O:O + 1], 0.5, None, ALU.mult))
                for k, dst in ((2, attW[:, P:P + 1]), (3, wa2[:, :])):
                    link(v.tensor_tensor(scr[:, :], attW[:, 0:P], rows_bc[:, k, :], ALU.mult))
                    link(v.tensor_reduce(dst, scr[:, :], AX_X, ALU.add))
                link(v.tensor_scalar(wa2_bc[:, :], ones[:, :], wa2[:, 0:1], None, ALU.mult))
                dve.sem_inc(consts_ready, 1)

            def norm_stats(k, stage, src, st_t, mv_t, c, inst, tag, first):
                done = sig[stage, "dve"][c]
                even, odd = st_t[c][:, :, 1:3], st_t[c][:, :, 4:6]
                if k == first:
                    for b in range(GB):
                        ins = v.bn_stats(st_t[c][:, b, :], src[c][:, b, :])
                    ins.then_inc(done, 1)
                if k == first + 1:
                    wait(dve, stage, "dve", c, "st" + tag, inst)
                    v.tensor_tensor(mv_t[c][:, :, 0:2], even, odd, ALU.add).then_inc(done, 1)
                    v.tensor_tensor(mv_t[c][:, :, 2], even[:, :, 0], odd[:, :, 0], ALU.subtract).then_inc(done, 1)
                if k == first + 2:
                    wait(dve, stage, "dve", c, "d" + tag, inst)
                    v.scalar_tensor_tensor(out=mv_t[c][:, :, 3], in0=mv_t[c][:, :, 2], scalar=0.25,
                                           in1=mv_t[c][:, :, 2], op0=ALU.mult, op1=ALU.mult)
                    v.tensor_scalar(mv_t[c][:, :, 4], mv_t[c][:, :, 1], 1.0 / P, EPS, ALU.mult, ALU.add)
                    v.tensor_scalar(mv_t[c][:, :, 5], mv_t[c][:, :, 0], 0.5, None, ALU.mult).then_inc(done, 1)
                if k == first + 3:
                    wait(dve, stage, "dve", c, "dd" + tag, inst)
                    v.tensor_tensor(mv_t[c][:, :, 6], mv_t[c][:, :, 3], mv_t[c][:, :, 4], ALU.add
                                    ).then_inc(done, 1)

            def normed(stage, dst, src, mv_t, rs_t, c, inst, tag):
                wait(dve, stage, "pool", c, "rs" + tag, inst)
                for b in range(GB):
                    ins = v.tensor_scalar(dst[c][:, b, :], src[c][:, b, :], mv_t[c][:, b, 5:6], rs_t[c][:, b:b + 1],
                                          ALU.subtract, ALU.mult)
                ins.then_inc(sig[stage, "dve"][c], 1)

            def gate(c, j):
                return gg[c][:, :, j:j + 1].to_broadcast([P, GB, P])

            def front(j, k, c, inst, before):
                done = sig["front", "dve"][c]
                if j == 0:
                    if k == 0:
                        dve.wait_ge(x_loaded[c], 16 * (inst + 1))
                    norm_stats(k, "front", xin, st, mv, c, inst, "0", first=0)
                if j == 1:
                    normed("front", xn, xin, mv, rs, c, inst, "0")
                if j == 3:
                    wait(dve, "front", "pe", c, "gates", inst)
                    v.tensor_tensor(gz[c][:, :, :], Rb[c][:, 0:3 * GB].rearrange("p (b k) -> p b k", k=3),
                                    gbias.rearrange("p (o k) -> p o k", o=1).to_broadcast([P, GB, 3]),
                                    ALU.add).then_inc(done, 1)
                if j == 4:
                    wait(dve, "front", "act", c, "tanh", inst)
                    v.tensor_scalar(gg[c][:, :, :], gt[c][:, :, :], 0.5, 0.5, ALU.mult, ALU.add).then_inc(done, 1)
                if j == 5 and k == 0:
                    wait(dve, "front", "dve", c, "g", inst)
                    wait(dve, "front", "pe", c, "in", inst)
                    v.tensor_tensor(u1[c][:, :, :], as_b(Ra[c]), gate(c, 0), ALU.mult).then_inc(done, 1)
                if j == 5 and k == 1:
                    wait(dve, "front", "pe", c, "out", inst)
                    v.tensor_tensor(u2[c][:, :, :], as_b(Rb[c]), gate(c, 1), ALU.mult).then_inc(done, 1)
                if j == 5 and k == 2:
                    wait(dve, "front", "dve", c, "u2", inst)
                    v.tensor_tensor(flat(u1[c]), flat(u1[c]), flat(u2[c]), ALU.add).then_inc(done, 1)
                if j == 6 and k == 0:
                    wait(dve, "front", "dve", c, "u", inst)
                    wait(dve, "front", "pool", c, "e", inst)
                    v.tensor_tensor(flat(u1[c]), flat(u1[c]), flat(e0[c]), ALU.add).then_inc(done, 1)
                if j == 6 and k == 1:
                    wait(dve, "front", "dve", c, "s", inst)
                    v.scalar_tensor_tensor(out=flat(x1[c]), in0=flat(u1[c]), scalar=0.0, in1=flat(xin[c]),
                                           op0=ALU.max, op1=ALU.add).then_inc(done, 1)
                if j == 6:
                    if k == 2:
                        wait(dve, "front", "dve", c, "x1", inst)
                    norm_stats(k, "front", x1, st, mv, c, inst, "1", first=2)
                if j == 7:
                    normed("front", xn, x1, mv, rs, c, inst, "1")
                if j in (8, 9):
                    b = 2 * (j - 8) + 1
                    wait(dve, "front", "pe", c, f"z{b}", inst)
                    v.tensor_copy(z[c][:, b, :, :], Rb[c][:, 0:3 * P].rearrange("p (k n) -> p k n", k=3)
                                  ).then_inc(done, 1)
                if j == 10 and k == 0:
                    wait(dve, "front", "pe", c, "sem", inst)
                    wait(dve, "front", "pool", c, "x1b", inst)
                    wait(dve, "lstm", "pool", c, "hold", inst - 1)
                    v.tensor_tensor(flat(x2[c]), Ra[c][:, :], flat(x1b[c]), ALU.add).then_inc(done, 1)
                if j == 10:
                    if k == 1:
                        wait(dve, "front", "dve", c, "x2", inst)
                    norm_stats(k, "front", x2, st, mv, c, inst, "2", first=1)
                if j == 11:
                    normed("front", xn, x2, mv, rs, c, inst, "2")

            def gcn(j, k, c, inst, before):
                done = sig["gcn", "dve"][c]
                if j == 2:
                    wait(dve, "gcn", "pe", c, "w1", inst)
                    v.tensor_tensor(y1[c], as_b(La[c]), over_b(rows_bc[:, 1, :]), ALU.add
                                    ).then_inc(done, 1)
                if j == 3:
                    wait(dve, "gcn", "act", c, "hin", inst)
                    v.scalar_tensor_tensor(out=flat(hinL[c]), in0=Lb[c][:, :], scalar=0.0, in1=flat(hinH[c]),
                                           op0=ALU.max, op1=ALU.subtract).then_inc(done, 1)

            def lstm(j, k, c, inst, before):
                done = sig["lstm", "dve"][c]
                p, s = LSTM_STEPS[j // 2]
                at, n = f"{p}.{s}", GB * (P // p)
                if j % 2 == 0:
                    if k == 0:
                        wait(dve, "lstm", "act", c, at + "g", inst)
                        v.scalar_tensor_tensor(out=(ig if s else c2)[c][:, 0:n], in0=ti[c][:, 0:n], scalar=1.0,
                                               in1=tg[c][:, 0:n], op0=ALU.add, op1=ALU.mult).then_inc(done, 1)
                    if k == 1:
                        wait(dve, "lstm", "act", c, at + "f", inst)
                        v.scalar_tensor_tensor(out=fc[c][:, 0:n], in0=tf[c][:, 0:n], scalar=1.0,
                                               in1=c2[c][:, 0:n], op0=ALU.add, op1=ALU.mult).then_inc(done, 1)
                    if k == 2:
                        wait(dve, "lstm", "dve", c, at + "fc", inst)
                        v.scalar_tensor_tensor(out=c2[c][:, 0:n], in0=fc[c][:, 0:n], scalar=0.5,
                                               in1=ig[c][:, 0:n], op0=ALU.mult, op1=ALU.add).then_inc(done, 1)
                else:
                    wait(dve, "lstm", "act", c, at + "tc", inst)
                    if p == 1:
                        wait(dve, "att", "pe", c, "h", inst - 1)
                    a, b = to[c][:, 0:n], tc[c][:, 0:n]
                    if s < p - 1:
                        dst = hs[c][:, 0:n]
                    else:
                        if p > 1:
                            wait(dve, "lstm", "pool", c, f"{p - 1}.{p - 2}L", inst)
                        dst = H[c][:, :, s:s + (P // p - 1) * p + 1:p]
                        a, b = (t.rearrange("p (b w) -> p b w", b=GB) for t in (a, b))
                    v.scalar_tensor_tensor(out=dst, in0=a, scalar=1.0, in1=b, op0=ALU.add, op1=ALU.mult
                                           ).then_inc(done, 1)

            def att(j, k, c, inst, before):
                done = sig["att", "dve"][c]
                if j == 0 and k == 0:
                    wait(dve, "att", "pe", c, "h", inst)
                    wait(dve, "lstm", "pool", c, "hold", inst)
                    v.scalar_tensor_tensor(out=flat(x3[c]), in0=Ra[c][:, :], scalar=0.5, in1=flat(x2h[c]),
                                           op0=ALU.mult, op1=ALU.add).then_inc(done, 1)
                if j == 0:
                    if k == 1:
                        wait(dve, "att", "dve", c, "x3", inst)
                    norm_stats(k, "att", x3, ast, amv, c, inst, "", first=1)
                if j == 1:
                    normed("att", axn, x3, amv, ars, c, inst, "")
                if j == 3:
                    wait(dve, "att", "pe", c, "wh23", inst)
                    v.tensor_copy(wh[c][:, 2:4, 0:P + 1], Rb[c][:, 0:2 * (P + 1)].rearrange("p (b k) -> p b k", b=2)
                                  ).then_inc(done, 1)
                if j == 4 and k == 0:
                    wait(dve, "att", "act", c, "wh", inst)
                    wait(dve, "att", "dve", c, "wh", inst)
                    wait(dve, "att", "pe", c, "z", inst)
                    v.tensor_tensor(ee[c][:, :, :], as_b(Ra[c]), wh[c][:, :, P:P + 1].to_broadcast([P, GB, P]),
                                    ALU.add).then_inc(done, 1)
                if j == 4 and k == 1:
                    wait(dve, "att", "dve", c, "ee", inst)
                    v.scalar_tensor_tensor(out=flat(pr[c]), in0=flat(ee[c]), scalar=ALPHA, in1=flat(ee[c]),
                                           op0=ALU.mult, op1=ALU.max).then_inc(done, 1)
                    v.tensor_reduce(n0[c][:, :], ee[c][:, :, :], AX_X, ALU.max, negate=True).then_inc(done, 1)
                if j == 4 and k == 2:
                    wait(dve, "att", "dve", c, "n0", inst)
                    v.scalar_tensor_tensor(out=nm[c][:, :], in0=n0[c][:, :], scalar=ALPHA, in1=n0[c][:, :],
                                           op0=ALU.mult, op1=ALU.min).then_inc(done, 1)
                if j == 7 and k < 2:
                    wait(dve, "att", "pe", c, ("num01", "num23")[k], inst)
                    v.reciprocal(rc[c][:, 2 * k:2 * k + 2, :], (Ra, Rb)[k][c][:, 0:2 * (P + 2)]
                                 .rearrange("p (b k) -> p b k", b=2)[:, :, P + 1:P + 2]).then_inc(done, 1)
                if j == 7 and k == 2:
                    wait(dve, "att", "dve", c, "r23", inst)
                    dve.wait_ge(out_free[c], 16 * (inst + 1))
                    for b in range(GB):
                        R = (Ra, Rb)[b // 2][c][:, b % 2 * (P + 2):b % 2 * (P + 2) + P]
                        ins = v.scalar_tensor_tensor(out=xo[c][:, b, :], in0=R, scalar=rc[c][:, b, 0:1],
                                                     in1=x3[c][:, b, :], op0=ALU.mult, op1=ALU.add)
                    ins.then_inc(done, 1)

            run(dve, "dve", {"front": front, "gcn": gcn, "lstm": lstm, "att": att}, late_from=100, late=late_constants)

        @block.scalar
        def _(act):
            a = nc.scalar.activation
            for dst, src in (
                (mats[:, :, :], sem_gcn_w.rearrange("k f o -> f k o")),
                (attW[:, 0:P], att_w), (lb[:, :, :, :], lstm_b.rearrange("k d p g -> d k p g")),
                (WihT[:, :, :], wih_t.rearrange("k d g -> d k g")),
                (WhhT[:, :, :], whh_t.rearrange("k d g -> d k g")),
            ):
                act.dma_start(dst, src).then_inc(weights_loaded, 16)
            act.wait_ge(weights_loaded, 16 * N_WEIGHTS)
            a(WihT[:, 1:, :], WihT[:, 1:, :], ACT.Copy, scale=0.5).then_inc(weights_scaled, 1)
            a(WhhT[:, :, :], WhhT[:, :, :], ACT.Copy, scale=0.5).then_inc(weights_scaled, 1)
            act.wait_ge(weights_scaled, 2)
            for k, p in enumerate((1, 2, 4)):
                a(WihH[:, k, :], WihT[:, p - 1, :], ACT.Copy).then_inc(weights_scaled, 1)
            act.wait_ge(graph_ready, 1)

            def late_constants():
                act.wait_ge(consts_ready, 1)


            def front(j, k, c, inst, before):
                done = sig["front", "act"][c]
                if j in (1, 7, 11) and k == 0:
                    tag = {1: "0", 7: "1", 11: "2"}[j]
                    wait(act, "front", "dve", c, "xn" + tag, inst)
                    if j == 1:
                        wait(act, "gcn", "pe", c, "q", inst - 1)
                    a(flat(h[c]), flat(xn[c]), ACT.Relu).then_inc(done, 1)
                if j == 7 and k == 1:
                    wait(act, "front", "act", c, "h1", inst)
                    a(flat(dh[c]), flat(h[c]), ACT.Copy, scale=diag[:, 0:1]).then_inc(done, 1)
                if j == 2:
                    wait(act, "front", "pe", c, "hT", inst)
                    a(flat(hT[c]), Ra[c][:, :], ACT.Copy).then_inc(done, 1)
                if j == 3:
                    wait(act, "front", "dve", c, "gz", inst)
                    a(gt[c][:, :, :], gz[c][:, :, :], ACT.Tanh, scale=0.5).then_inc(done, 1)
                if j == 4:
                    wait(act, "front", "dve", c, "g", inst)
                    for b in range(GB):
                        ins = a(e2[c][:, b, :], h[c][:, b, :], ACT.Copy, scale=gg[c][:, b, 2:3])
                    ins.then_inc(done, 1)
                if j in (8, 9):
                    b = 2 * (j - 8)
                    wait(act, "front", "pe", c, f"z{b}", inst)
                    a(z[c][:, b, :, :], Ra[c][:, 0:3 * P].rearrange("p (k n) -> p k n", k=3), ACT.Copy
                      ).then_inc(done, 1)

            def gcn(j, k, c, inst, before):
                done = sig["gcn", "act"][c]
                if j == 0:
                    wait(act, "gcn", "pe", c, "q", inst)
                    wait(act, "lstm", "dve", c, "4.3h", inst - 1)
                    a(flat(q[c]), La[c][:, :], ACT.Copy).then_inc(done, 1)
                if j == 1:
                    wait(act, "gcn", "pe", c, "w0", inst)
                    a(flat(y0[c]), Lb[c][:, :], ACT.Relu).then_inc(done, 1)
                if j == 3:
                    wait(act, "gcn", "pe", c, "w2", inst)
                    wait(act, "lstm", "pe", c, "1.0o", inst - 1)
                    a(flat(hinH[c]), Lb[c][:, :], ACT.Relu).then_inc(done, 1)

            def lstm(j, k, c, inst, before):
                done = sig["lstm", "act"][c]
                p, s = LSTM_STEPS[j // 2]
                at, n = f"{p}.{s}", GB * (P // p)

                def gate(dst, src, which):
                    a(dst[c][:, 0:n], src, ACT.Tanh, bias=gb[:, p - 1, which:which + 1],
                      scale=1.0 if which == G else 0.5).then_inc(done, 1)

                if p == 1:
                    if j % 2 == 0 and k == 0:
                        wait(act, "lstm", "pe", c, at + "i", inst)
                        gate(ti, La[c][:, :], I)
                    if j % 2 == 0 and k == 1:
                        wait(act, "lstm", "pe", c, at + "g", inst)
                        gate(tg, Lb[c][:, :], G)
                    if j % 2 and k == 0:
                        wait(act, "lstm", "pe", c, at + "o", inst)
                        gate(to, La[c][:, :], O)
                elif j % 2 == 0:
                    at_0 = s % 2 * n if p == MAX_SKIP else 0
                    at_1 = COLS // 2 + at_0
                    if k == 0:
                        wait(act, "lstm", "pe", c, at + "ig", inst)
                        gate(ti, La[c][:, at_0:at_0 + n], I)
                        gate(tg, La[c][:, at_1:at_1 + n], G)
                    if k == 1:
                        wait(act, "lstm", "pe", c, at + "fo", inst)
                        if s:
                            gate(tf, Lb[c][:, at_0:at_0 + n], F)
                        gate(to, Lb[c][:, at_1:at_1 + n], O)
                if j % 2 and k == (1 if p == 1 else 0):
                    wait(act, "lstm", "dve", c, at + "c", inst)
                    a(tc[c][:, 0:n], c2[c][:, 0:n], ACT.Tanh, scale=0.5).then_inc(done, 1)
                if j % 2 and k == (2 if p == 1 else 1):
                    last = slice(s, s + (P // p - 1) * p + 1, p)
                    wait(act, "lstm", "dve", c, at + "h", inst)
                    a(HH[c][:, :, last], H[c][:, :, last], ACT.Copy).then_inc(done, 1)

            def att(j, k, c, inst, before):
                done = sig["att", "act"][c]
                if j == 1:
                    wait(act, "att", "dve", c, "xn", inst)
                    a(flat(ah[c]), flat(axn[c]), ACT.Relu).then_inc(done, 1)
                if j == 2:
                    wait(act, "att", "pe", c, "hT", inst)
                    a(flat(ahT[c]), Rb[c][:, :], ACT.Copy).then_inc(done, 1)
                if j == 3:
                    wait(act, "att", "pe", c, "wh01", inst)
                    a(wh[c][:, 0:2, 0:P + 1], Ra[c][:, 0:2 * (P + 1)].rearrange("p (b k) -> p b k", b=2), ACT.Copy
                      ).then_inc(done, 1)
                if j == 5:
                    wait(act, "att", "dve", c, "nm", inst)
                    for b in range(GB):
                        ins = a(ee[c][:, b, :], pr[c][:, b, :], ACT.Exp, bias=nm[c][:, b:b + 1])
                    ins.then_inc(done, 1)
                if j == 6:
                    wait(act, "att", "pe", c, "aT", inst)
                    a(flat(aT[c]), Rb[c][:, :], ACT.Copy).then_inc(done, 1)

            run(act, "act", {"front": front, "gcn": gcn, "lstm": lstm, "att": att}, late_from=110, late=late_constants)

        @block.tensor
        def _(pe):
            mm_ = nc.tensor.matmul
            pe.wait_ge(graph_loaded, 16 * N_GRAPH)
            pe.wait_ge(pool_const, N_POOL_CONST)
            mm_(bank[0][0:1, 0:P], ones[:, 0:1], adjT, start=True, stop=True).then_inc(pe_const, 1)
            mm_(bank[1][:, :], ones[0:1, :], rows_t[0:1, 0:4, :].rearrange("p k d -> p (k d)"), start=True, stop=True
                ).then_inc(pe_const, 1)
            pe.wait_ge(graph_ready, 1)

            def late_constants():
                pe.wait_ge(weights_loaded, 16 * N_WEIGHTS)
                pe.wait_ge(consts_ready, 1)
                pe.wait_ge(pairs_moved, 32)


            def bank_free(c, which, before):
                if before is not None:
                    stage, inst = before
                    who, step = {("front", "a"): ("dve", "x2"), ("front", "b"): ("dve", "z3"),
                                 ("att", "a"): ("dve", "out"), ("att", "b"): ("dve", "out")}[stage, which]
                    wait(pe, stage, who, c, step, inst)

            def front(j, k, c, inst, before):
                done = sig["front", "pe"][c]
                if j == 2:
                    wait(pe, "front", "act", c, "h0", inst)
                    bank_free(c, "a", before)
                    for b in range(GB):
                        ins = nc.tensor.transpose(Ra[c][:, b * P:(b + 1) * P], h[c][:, b, :], ident[:, :])
                    ins.then_inc(done, 1)
                if j == 3:
                    wait(pe, "front", "act", c, "hT", inst)
                    bank_free(c, "b", before)
                    for b in range(GB):
                        ins = mm_(Rb[c][:, 3 * b:3 * b + 3], hT[c][:, b, :], gvec, start=True, stop=True)
                    ins.then_inc(done, 1)
                if j == 4 and k == 0:
                    mm_(Ra[c][:, :], a_in[:, :], flat(h[c]), start=True, stop=True).then_inc(done, 1)
                if j == 4 and k == 1:
                    wait(pe, "front", "dve", c, "gz", inst)
                    mm_(Rb[c][:, :], a_out[:, :], flat(h[c]), start=True, stop=True).then_inc(done, 1)
                if j in (8, 9):
                    for b, R in {8: ((0, Ra), (1, Rb)), 9: ((2 + k, (Ra, Rb)[k]),)}[j]:
                        if b == 0:
                            wait(pe, "front", "act", c, "dh", inst)
                        if b == 2:
                            wait(pe, "front", "act", c, "z0", inst)
                        if b == 3:
                            wait(pe, "front", "dve", c, "z1", inst)
                        nc.tensor.transpose(R[c][:, 0:P], dh[c][:, b, :], ident[:, :])
                        mm_(R[c][:, P:3 * P], h[c][:, b, :], a_sem[:, :, :].rearrange("p k n -> p (k n)"),
                            start=True, stop=True).then_inc(done, 1)
                if j == 10:
                    wait(pe, "front", "act", c, "z2", inst)
                    wait(pe, "front", "dve", c, "z3", inst)
                    for b in range(GB):
                        for k in range(3):
                            ins = mm_(Ra[c][:, b * P:(b + 1) * P], z[c][:, b, k, :], semW[:, k, :],
                                      start=k == 0, stop=k == 2)
                    ins.then_inc(done, 1)

            def gcn(j, k, c, inst, before):
                done = sig["gcn", "pe"][c]
                if j == 0:
                    wait(pe, "front", "act", c, "h2", inst)
                    wait(pe, "lstm", "act", c, "4.3o", inst - 1)
                    for b in range(GB):
                        ins = mm_(La[c][:, b * P:(b + 1) * P], h[c][:, b, :], adjT, start=True, stop=True)
                    ins.then_inc(done, 1)
                if j == 1:
                    wait(pe, "gcn", "act", c, "q", inst)
                    mm_(Lb[c][:, :], Wg[:, 0, :], flat(q[c]), start=True, stop=False)
                    mm_(as_b(Lb[c]), bg0_9[0:9, :], rs_9[0:9, :].rearrange("p (o n) -> p o n", o=1)
                        .to_broadcast([9, GB, P]), start=False, stop=True).then_inc(done, 1)
                if j == 2:
                    wait(pe, "gcn", "act", c, "y0", inst)
                    for b in range(GB):
                        ins = mm_(La[c][:, b * P:(b + 1) * P], y0[c][:, b, :], Wg[:, 1, :], start=True, stop=True)
                    ins.then_inc(done, 1)
                if j == 3:
                    wait(pe, "gcn", "dve", c, "y1", inst)
                    for b in range(GB):
                        ins = mm_(Lb[c][:, b * P:(b + 1) * P], y1[c][:, b, :], adjT, start=True, stop=True)
                    ins.then_inc(done, 1)

            def lstm(j, k, c, inst, before):
                done = sig["lstm", "pe"][c]
                p, s = LSTM_STEPS[j // 2]
                at, nw = f"{p}.{s}", P // p
                n = GB * nw
                def halves(k, which, xH, xL):
                    cols = slice(which * P, (which + 1) * P)
                    return ((WihH[:, k, cols], xH), (WihL[:, k, cols], xH), (WihH[:, k, cols], xL))

                if p == 1:
                    def product(R, which):
                        for m, (w, x_) in enumerate(halves(0, which, flat(hinH[c]), flat(hinL[c]))):
                            if m == 2 and which == I:
                                wait(pe, "gcn", "dve", c, "hinL", inst)
                            ins = mm_(R[c][:, :], w, x_, start=m == 0, stop=m == 2)
                        ins.then_inc(done, 1)
                    if j % 2 == 0:
                        if isinstance(inst, int) and inst == 0:
                            pe.wait_ge(weights_split, 3)
                        wait(pe, "gcn", "act", c, "hin", inst)
                        product(La, I)
                        product(Lb, G)
                    else:
                        wait(pe, "lstm", "act", c, at + "i", inst)
                        product(La, O)
                    return

                def gates(first):
                    at_0 = s % 2 * n if p == MAX_SKIP else 0
                    for which, R, col in ((I, La, 0), (G, La, COLS // 2), (F, Lb, 0), (O, Lb, COLS // 2)):
                        if not (first and which == F):
                            yield which, R[c][:, col + at_0:col + at_0 + n]

                def opens(which, at_s):
                    return which in (I, F) or (which == O and at_s == 0 and p < MAX_SKIP)

                def from_x(at_s):
                    last = slice(at_s, at_s + (nw - 1) * p + 1, p)
                    for which, dst in gates(at_s == 0):
                        dst = dst.rearrange("p (b w) -> p b w", b=GB)
                        if p == 3:
                            passes = ((WihT[:, p - 1, which * P:(which + 1) * P], H[c][:, :, last]),)
                        else:
                            passes = halves(1, which, HH[c][:, :, last], HL[c][:, :, last])
                        for m, (w, x_) in enumerate(passes):
                            if at_s == 0 and which == I and m == 2:
                                wait(pe, "lstm", "pool", c, f"{p - 1}.{p - 2}L", inst)
                            ins = mm_(dst, w, x_, start=m == 0 and opens(which, at_s),
                                      stop=at_s == 0 and m == len(passes) - 1, skip_group_check=True)
                        if at_s == 0 and which in (G, O):
                            ins.then_inc(done, 1)

                def from_x_pair(at_s):
                    xs = [t[c][:, :, :].rearrange("p b (w k) -> p k b w", k=p)[:, at_s:at_s + 2] for t in (HH, HL)]
                    for which, R, col in ((I, La, 0), (G, La, COLS // 2), (F, Lb, 0), (O, Lb, COLS // 2)):
                        dst = R[c][:, col:col + 2 * n].rearrange("p (k b w) -> p k b w", k=2, b=GB)
                        for m, (w, x_) in enumerate(halves(2, which, *xs)):
                            if at_s == 0 and which == I and m == 2:
                                wait(pe, "lstm", "pool", c, f"{p - 1}.{p - 2}L", inst)
                            ins = mm_(dst, w, x_, start=m == 0 and which in (I, F), stop=at_s == 0 and m == 2,
                                      skip_group_check=True)
                        if at_s == 0 and which in (G, O):
                            ins.then_inc(done, 1)

                if p == MAX_SKIP and j % 2 == 0 and s == 0:
                    wait(pe, "lstm", "act", c, f"{p - 1}.{p - 2}H", inst)
                    from_x_pair(0)
                elif p == MAX_SKIP and j % 2:
                    if s == 1:
                        wait(pe, "lstm", "act", c, at + "o", inst)
                        from_x_pair(2)
                elif p == 2 and j % 2 == 0 and s == 0:
                    wait(pe, "lstm", "act", c, "1.0H", inst)
                    from_x(0)
                elif j % 2 == 0 and s == 0:
                    wait(pe, "lstm", "dve", c, f"{p - 1}.{p - 2}h", inst)
                    from_x(0)
                elif j % 2 == 0:
                    wait(pe, "lstm", "dve", c, f"{p}.{s - 1}h", inst)
                    for which, dst in gates(False):
                        ins = mm_(dst, WhhT[:, p - 2, which * P:(which + 1) * P], hs[c][:, 0:n], start=False,
                                  stop=True, skip_group_check=True)
                        if which in (G, O):
                            ins.then_inc(done, 1)
                elif s + 1 < p:
                    wait(pe, "lstm", "act", c, at + "o", inst)
                    from_x(s + 1)

            def att(j, k, c, inst, before):
                done = sig["att", "pe"][c]
                if j == 0:
                    wait(pe, "lstm", "dve", c, "4.3h", inst)
                    bank_free(c, "a", before)
                    for b in range(GB):
                        ins = nc.tensor.transpose(Ra[c][:, b * P:(b + 1) * P], H[c][:, b, :], ident[:, :])
                    ins.then_inc(done, 1)
                if j == 2:
                    wait(pe, "att", "act", c, "h3", inst)
                    bank_free(c, "b", before)
                    for b in range(GB):
                        ins = nc.tensor.transpose(Rb[c][:, b * P:(b + 1) * P], ah[c][:, b, :], ident[:, :])
                    ins.then_inc(done, 1)
                if j == 3:
                    wait(pe, "att", "act", c, "hT", inst)
                    for R, b0 in ((Ra, 0), (Rb, 2)):
                        for b in (0, 1):
                            ins = mm_(R[c][:, b * (P + 1):(b + 1) * (P + 1)], ahT[c][:, b0 + b, :], attW[:, 0:P + 1],
                                      start=True, stop=True)
                        ins.then_inc(done, 1)
                if j == 4:
                    wait(pe, "att", "act", c, "wh", inst)
                    mm_(Ra[c][:, :], wa2_bc[:, :], flat(ahT[c]), start=True, stop=False)
                    mm_(as_b(Ra[c]), identb[:, :], over_b(maskb[:, :]), start=False, stop=True).then_inc(done, 1)
                if j == 6:
                    wait(pe, "att", "act", c, "p", inst)
                    wait(pe, "att", "dve", c, "wh", inst)
                    for b in range(GB):
                        ins = nc.tensor.transpose(Rb[c][:, b * P:(b + 1) * P], ee[c][:, b, :], ident[:, :])
                    ins.then_inc(done, 1)
                if j == 7:
                    wait(pe, "att", "act", c, "aT", inst)
                    for b in (0, 1):
                        ins = mm_((Ra, Rb)[k][c][:, b * (P + 2):(b + 1) * (P + 2)], aT[c][:, 2 * k + b, :],
                                  wh[c][:, 2 * k + b, :], start=True, stop=True)
                    ins.then_inc(done, 1)

            run(pe, "pe", {"front": front, "gcn": gcn, "lstm": lstm, "att": att}, late_from=100, late=late_constants)


def kernel(**inputs):
    import numpy as np
    import concourse.bacc as bacc
    from concourse.bass_utils import run_bass_kernel_spmd

    t = {name: np.asarray(a) for name, a in inputs.items()}
    lstm_b = [t[f"L2_gnn_{b}"].reshape(MAX_SKIP, 4, P).transpose(2, 0, 1) for b in ("bih", "bhh")]
    arrays = {
        "x": t["x"],
        "graph": np.stack([t["adj"].T, t["adj"], t["L0_gnn_edge_bias"], t["L0_gnn_out_edge_bias"]]),
        "gate_cols": np.concatenate([t["L0_gnn_gate_weight"], t["L0_gnn_out_gate_weight"], t["L0_gnn_loop_gate"],
                                     t["L0_gnn_bias_gate"], t["L0_gnn_out_bias_gate"],
                                     np.zeros((P, 1), np.float32)], axis=1),
        "rows": np.stack([t["L1_gnn_bias"], t["L2_gnn_bg1"], t["L3_gnn_a"][:P, 0], t["L3_gnn_a"][P:, 0],
                          t["L2_gnn_bg0"]])[None],
        "sem_gcn_w": np.concatenate([t["L1_gnn_W"], t["L2_gnn_Wg0"][None], t["L2_gnn_Wg1"][None]]),
        "wih_t": t["L2_gnn_Wih"].transpose(0, 2, 1),
        "whh_t": t["L2_gnn_Whh"][1:].transpose(0, 2, 1),
        "lstm_b": np.stack(lstm_b),
        "att_w": t["L3_gnn_W"],
    }
    arrays = {f"in_{name}": np.ascontiguousarray(a) for name, a in arrays.items()}
    nc = bacc.Bacc("TRN2", target_bir_lowering=False, num_devices=1)
    aps = [nc.dram_tensor(name, a.shape, mybir.dt.from_np(a.dtype), kind="ExternalInput").ap()
           for name, a in arrays.items()]
    out = nc.dram_tensor("out", t["x"].shape, F32, kind="ExternalOutput").ap()
    graph_layers_kernel(nc, *aps, out)
    return run_bass_kernel_spmd(nc, [arrays], core_ids=[0]).results[0]["out"]
```

```python
from contextlib import ExitStack

import concourse.bass as bass
from concourse import mybir

F32 = mybir.dt.float32
F32R = mybir.dt.float32r
BF16 = mybir.dt.bfloat16
ALU = mybir.AluOpType
ACT = mybir.ActivationFunctionType
AX_X = mybir.AxisListType.X

P = 128
GB = 4
CHAINS = 2
COLS = GB * P
MAX_SKIP = 4
EPS = 1e-5
ALPHA = 0.2
MASKED = -float(2 ** 100)
I, F, G, O = range(4)

LSTM_STEPS = [(p, s) for p in range(1, MAX_SKIP + 1) for s in range(p)]


def _lstm_names():
    pe, act, dve, pool = [], [], [], []
    for p, s in LSTM_STEPS:
        at = f"{p}.{s}"
        if p == 1:
            pe += [at + "i", at + "g", at + "o"]
            act += [at + "i", at + "g", at + "o", at + "tc", at + "H"]
            pool += [at + "L"]
            dve += [at + "c", at + "h"]
        else:
            pe += [at + "ig", at + "fo"]
            act += [at + "i", at + "g"] + ([at + "f"] if s else []) + [at + "o", at + "tc"]
            dve += ([at + "ig", at + "fc"] if s else []) + [at + "c", at + "h"]
            if 1 < p < MAX_SKIP and s == p - 1 or p == 2:
                act += [at + "H"]
                pool += [at + "L"]
    return pe, act, dve, pool


ROUND = 100000
LAG = 49988
PLACES = {
    "pe": {
        "front": {20: -46388, 30: -44758, 40: -35497, 41: -35496, 80: -2181, 90: -1374, 91: -1373, 100: 1566},
        "gcn": {0: 15488, 10: 21805, 20: 26278, 30: 28158},
        "lstm": {0: 31058, 10: 31337, 20: 43737, 30: 48146, 40: 49916, 60: 54152, 70: 55336, 80: 55337, 90: 69779,
                 100: 74076, 120: 78458, 140: 90158, 150: 91438, 160: 94817, 180: 100061},
        "att": {0: 104366, 20: 127456, 30: 133220, 40: 140593, 60: 148699, 70: 149979, 71: 149980},
    },
    "act": {
        "front": {10: -48601, 11: -45558, 20: -41049, 30: -36196, 40: -33214, 70: -15690, 71: -13628, 72: -13627,
                  80: -2740, 90: -970, 110: 14096},
        "gcn": {0: 16584, 10: 18239, 30: 24649},
        "lstm": {0: 27386, 1: 27812, 10: 30058, 11: 30416, 12: 32890, 20: 37645, 21: 39988, 30: 47782, 31: 47956,
                 40: 51150, 41: 51151, 50: 51606, 51: 54442, 60: 62469, 61: 62470, 70: 62471, 80: 64069, 81: 66149,
                 90: 66606, 100: 69810, 101: 70655, 110: 73966, 111: 74069, 120: 75630, 121: 77365, 130: 79346,
                 140: 81816, 141: 81817, 150: 85101, 160: 90544, 161: 98904, 170: 100394, 180: 101665, 181: 101801,
                 190: 105977},
        "att": {10: 123374, 20: 124934, 30: 130760, 50: 147936, 60: 149783},
    },
    "dve": {
        "front": {0: -72692, 1: -70419, 2: -70237, 3: -69170, 10: -64084, 30: -49960, 40: -49155, 50: -42115,
                  51: -41637, 52: -40718, 60: -34585, 61: -34584, 62: -29879, 63: -29878, 64: -29877, 65: -29607,
                  70: -24027, 80: -18936, 90: -16331, 100: -6997, 101: -4723, 102: -4722, 103: -4351, 104: -4350,
                  110: 4845},
        "gcn": {20: 14025, 30: 17096},
        "lstm": {0: 23247, 10: 26202, 20: 29032, 30: 31193, 40: 36654, 41: 38846, 42: 40177, 50: 42767, 60: 45472,
                 70: 49340, 80: 55572, 81: 55573, 82: 55715, 90: 58631, 100: 59810, 101: 61972, 102: 61973,
                 110: 64648, 120: 71006, 130: 75643, 140: 76609, 141: 76610, 142: 76611, 150: 78014, 160: 82084,
                 161: 83544, 162: 83556, 170: 84143, 180: 92893, 181: 92981, 182: 92982, 190: 93084},
        "att": {0: 100067, 1: 105330, 2: 105421, 3: 105622, 4: 107803, 10: 108983, 30: 126567, 40: 127335,
                41: 128030, 42: 128031, 70: 136190, 71: 139113, 72: 141183},
    },
    "pool": {
        "front": {0: -54200, 10: -48683, 40: -35359, 41: -29770, 50: -23273, 60: -17395, 70: -11553, 100: 8818},
        "lstm": {10: 36573, 30: 42460, 31: 61145, 50: 70668, 110: 78505},
        "att": {0: 119321},
    },
}
_LPE, _LACT, _LDVE, _LPOOL = _lstm_names()

STEPS = {
    "front": {
        "pe": ["hT", "gates", "in", "out", "z0", "z1", "z2", "z3", "sem"],
        "act": ["h0", "h0H", "hT", "tanh", "e2", "h1", "dh", "h1H", "z0", "z2", "h2"],
        "dve": ["st0", "sv0", "d0", "dd0", "mv0", "xn0", "gz", "g", "u1", "u2", "u", "s", "x1", "st1", "sv1", "d1", "dd1", "mv1", "xn1", "z1", "z3",
                "x2", "st2", "sv2", "d2", "dd2", "mv2", "xn2"],
        "pool": ["rs0", "h0L", "e0", "e1", "e01", "e", "rs1", "x1b", "h1L", "rs2"],
    },
    "gcn": {"pe": ["q", "w0", "w1", "w2"], "act": ["q", "y0", "hin"], "dve": ["y1", "hinL"]},
    "lstm": {"pe": _LPE, "act": _LACT, "dve": _LDVE, "pool": _LPOOL[:2] + ["hold"] + _LPOOL[2:]},
    "att": {
        "pe": ["h", "hT", "wh01", "wh23", "z", "aT", "num01", "num23"],
        "act": ["h3", "hT", "wh", "p", "aT"],
        "dve": ["x3", "st", "sv", "d", "dd", "mv", "xn", "wh", "ee", "lr", "n0", "nm", "r01", "r23", "out"],
        "pool": ["rs"],
    },
}


def graph_layers_kernel(nc, x, graph, gate_cols, rows, sem_gcn_w, wih_t, whh_t, lstm_b, att_w, out):
    B, N, D = x.shape
    assert N == P and D == P and B % (GB * CHAINS) == 0
    ROUNDS = B // (GB * CHAINS)
    assert ROUNDS >= 4

    ctx = ExitStack()
    with ctx:
        def sb(name, shape, dt=F32):
            return ctx.enter_context(nc.sbuf_tensor(name, [P] + shape, dt))

        def per_chain(name, shape, dt=F32):
            return [sb(f"{name}_{c}", shape, dt) for c in range(CHAINS)]

        def sem(name):
            return ctx.enter_context(nc.semaphore(name))

        graph_t = sb("graph_t", [4, P])
        adjT = graph_t[:, 0, :]
        adj_n = graph_t[:, 1, :]
        eb = graph_t[:, 2, :]
        oeb = graph_t[:, 3, :]
        a_in = sb("a_in", [P])
        a_out = sb("a_out", [P])
        a_sem = sb("a_sem", [2, P])
        a_inH, a_inL = sb("a_inH", [P], F32R), sb("a_inL", [P], F32R)
        a_outH, a_outL = sb("a_outH", [P], F32R), sb("a_outL", [P], F32R)
        a_semH, a_semL = sb("a_semH", [2, P], F32R), sb("a_semL", [2, P], F32R)
        diag = sb("diag", [1])
        org = sb("org", [P])
        gate_t = sb("gate_t", [6])
        gvec = gate_t[:, 0:3]
        gbias = gate_t[:, 3:6]
        rows_t = sb("rows_t", [5, P])
        rows_bc = sb("rows_bc", [4, P])
        mats = sb("mats", [5, P])
        semW = mats[:, 0:3, :]
        Wg = mats[:, 3:5, :]
        WihT = sb("WihT", [MAX_SKIP, 4 * P])
        WihH = sb("WihH", [3, 4 * P], F32R)
        WihL = sb("WihL", [3, 4 * P], F32R)
        WhhH = sb("WhhH", [4 * P], F32R)
        WhhL = sb("WhhL", [4 * P], F32R)
        WhhT = sb("WhhT", [MAX_SKIP - 1, 4 * P])
        lb = sb("lb", [2, MAX_SKIP, 4])
        gb = sb("gb", [MAX_SKIP, 4])
        attW = sb("attW", [P + 2])
        wa2 = sb("wa2", [1])
        wa2_bc = sb("wa2_bc", [P])
        scr = sb("scr", [P])
        ident = sb("ident", [P])
        identb = sb("identb", [P], BF16)
        ones = sb("ones", [P])
        zero = sb("zero", [P])
        maskb = sb("maskb", [P], BF16)
        half = sb("half", [GB])
        part = sb("part", [2, 3, P], BF16)
        rest = sb("rest", [2, P])
        pairs_row = sb("pairs_row", [2, 9, P], BF16)
        bg0_9 = sb("bg0_9", [P], BF16)
        rs_9 = sb("rs_9", [P], BF16)

        xin = per_chain("xin", [GB, P])
        st = per_chain("st", [GB, 6])
        mv = per_chain("mv", [GB, 7])
        rs = per_chain("rs", [GB])
        xn = per_chain("xn", [GB, P])
        h = per_chain("h", [GB, P])
        hH = per_chain("hH", [GB, P], F32R)
        hL = per_chain("hL", [GB, P], F32R)
        gz = per_chain("gz", [GB, 3])
        gt = per_chain("gt", [GB, 3])
        gg = per_chain("gg", [GB, 3])
        e0 = per_chain("e0", [GB, P])
        e1 = per_chain("e1", [GB, P])
        hT = e1
        e2 = per_chain("e2", [GB, P])
        u1 = per_chain("u1", [GB, P])
        u2 = per_chain("u2", [GB, P])
        x1 = per_chain("x1", [GB, P])
        x1b = e0
        dh = e2
        z = per_chain("z", [GB, 3, P])
        x2 = per_chain("x2", [GB, P])
        x2h = per_chain("x2h", [GB, P])
        hinH = per_chain("hinH", [GB, P], F32R)
        hinL = per_chain("hinL", [GB, P], F32R)
        ti = per_chain("ti", [COLS])
        tg = per_chain("tg", [COLS])
        tf = per_chain("tf", [COLS // 2])
        to = per_chain("to", [COLS])
        c2 = per_chain("c2", [COLS])
        ig = per_chain("ig", [COLS // 2])
        fc = per_chain("fc", [COLS // 2])
        tc = per_chain("tc", [COLS])
        q, y0, y1 = ([t[c][:, :].rearrange("p (b n) -> p b n", b=GB) for c in range(CHAINS)] for t in (ti, tg, tc))
        hs = per_chain("hs", [COLS // 2])
        hsH = per_chain("hsH", [COLS // 2], F32R)
        hsL = per_chain("hsL", [COLS // 2], F32R)
        H = per_chain("H", [GB, P])
        HH = per_chain("HH", [GB, P], F32R)
        HL = per_chain("HL", [GB, P], F32R)
        x3 = per_chain("x3", [GB, P])
        ast = per_chain("ast", [GB, 6])
        amv = per_chain("amv", [GB, 7])
        ars = per_chain("ars", [GB])
        axn = per_chain("axn", [GB, P])
        ah = per_chain("ah", [GB, P])
        ahT = per_chain("ahT", [GB, P])
        wh = per_chain("wh", [GB, P + 2])
        n0 = per_chain("n0", [GB])
        nm = per_chain("nm", [GB])
        ee = per_chain("ee", [GB, P])
        pr = per_chain("pr", [GB, P])
        aT = ahT
        rc = per_chain("rc", [GB, 1])
        xo = per_chain("xo", [GB, P])

        bank = [ctx.enter_context(nc.psum_tensor(f"bank{i}", [P, COLS], F32)) for i in range(8)]
        La, Lb = [bank[0], bank[2]], [bank[1], bank[3]]
        Ra, Rb = [bank[4], bank[6]], [bank[5], bank[7]]

        sig = {(stage, eng): [sem(f"{stage}_{eng}_{c}") for c in range(CHAINS)]
               for stage in STEPS for eng in STEPS[stage]}
        x_loaded = [sem(f"x_loaded_{c}") for c in range(CHAINS)]
        out_free = [sem(f"out_free_{c}") for c in range(CHAINS)]
        graph_loaded = sem("graph_loaded")
        weights_loaded = sem("weights_loaded")
        pool_const = sem("pool_const")
        dve_const = sem("dve_const")
        pe_const = sem("pe_const")
        pairs_ready = sem("pairs_ready")
        pairs_moved = sem("pairs_moved")
        graph_ready = sem("graph_ready")
        weights_scaled = sem("weights_scaled")
        weights_split = sem("weights_split")
        consts_ready = sem("consts_ready")

        def wait(eng, stage, who, c, step, inst):
            steps = STEPS[stage][who]
            value = inst * len(steps) + (steps.index(step) + 1)
            if not (isinstance(value, int) and value <= 0):
                eng.wait_ge(sig[stage, who][c], value)

        def over_b(t):
            return t.rearrange("p (o d) -> p o d", o=1).to_broadcast([P, GB, P])

        def flat(t):
            return t[:, :, :].rearrange("p b d -> p (b d)")

        def as_b(t):
            return t[:, :].rearrange("p (b d) -> p b d", d=P)

        N_GRAPH, N_WEIGHTS = 3, 5
        N_POOL_CONST = 5 + CHAINS
        block = ctx.enter_context(nc.Block())

        LAST = ROUNDS - 1

        def run(eng, name, parts, late_from=None, late=None):
            def part(stage, j, c, inst):
                inner = not isinstance(inst, int)
                if (stage, j, c) == ("front", late_from, 0) and not inner and inst == 0:
                    late()
                before = {"att": ("front", inst + 1) if inner or inst + 1 < ROUNDS else ("att", inst - 1),
                          "front": ("att", inst - 2) if inner or inst >= 2 else ("front", 0) if inst == 1 else None,
                          "gcn": None, "lstm": None}[stage]
                parts[stage](j // 10, j % 10, c, inst, before)

            order = []
            for stage, places in PLACES[name].items():
                for j, place in places.items():
                    for c in range(CHAINS):
                        at = place + c * LAG
                        order.append((at % ROUND, at // ROUND, stage, j, c))
            order.sort()
            begin, tail = min(o[1] for o in order), max(o[1] for o in order)

            def a_round(r):
                for _, behind, stage, j, c in order:
                    if not isinstance(r, int) or 0 <= r - behind < ROUNDS:
                        part(stage, j, c, r - behind)

            first, end = tail + 2, ROUNDS - 1 + begin
            for r in range(begin, first):
                a_round(r)
            with eng.Fori(first, end) as r:
                a_round(r)
            for r in range(end, ROUNDS + tail):
                a_round(r)

        @block.sync
        def _(sp):
            def load(c, inst):
                wait(sp, "front", "dve", c, "x1", inst - 1)
                first = (inst * CHAINS + c) * GB
                sp.dma_start(xin[c][:, :, :], x[bass.ds(first, GB), :, :].rearrange("b n d -> n b d")
                             ).then_inc(x_loaded[c], 16)

            def store(c, inst):
                wait(sp, "att", "dve", c, "out", inst)
                first = (inst * CHAINS + c) * GB
                sp.dma_start(out[bass.ds(first, GB), :, :].rearrange("b n d -> n b d"), xo[c][:, :, :]
                             ).then_inc(out_free[c], 16)

            for c in range(CHAINS):
                sp.sem_inc(out_free[c], 16)
            load(0, 0)
            for dst, src in (
                (gate_t[:, :], gate_cols),
                (graph_t[:, :, :], graph.rearrange("k i j -> i k j")),
                (rows_t[0:1, :, :], rows),
            ):
                sp.dma_start(dst, src).then_inc(graph_loaded, 16)
            load(1, 0)
            sp.wait_ge(pairs_ready, 1)
            sp.dma_start(bg0_9[0:9, :], pairs_row[0:1, 0, :, :]).then_inc(pairs_moved, 16)
            sp.dma_start(rs_9[0:9, :], pairs_row[0:1, 1, :, :]).then_inc(pairs_moved, 16)

            for c in range(CHAINS):
                load(c, 1)
            with sp.Fori(1, ROUNDS - 1) as k:
                for c in range(CHAINS):
                    load(c, k + 1)
                for c in range(CHAINS):
                    store(c, k - 1)
            for inst in (ROUNDS - 2, ROUNDS - 1):
                for c in range(CHAINS):
                    store(c, inst)
            for c in range(CHAINS):
                sp.wait_ge(out_free[c], 16 * (ROUNDS + 1))

        @block.gpsimd
        def _(pool):
            g = nc.gpsimd
            g.memset(zero[:, :], 0.0).then_inc(pool_const, 1)
            g.memset(ones[:, :], 1.0).then_inc(pool_const, 1)
            for c in range(CHAINS):
                g.memset(wh[c][:, :, P + 1:P + 2], 1.0).then_inc(pool_const, 1)
            pool.wait_ge(pool_const, 2 + CHAINS)
            g.affine_select(out=ident[:, :], in_=zero[:, :], compare_op=ALU.not_equal, fill=1.0, base=0,
                            pattern=[[-1, P]], channel_multiplier=1).then_inc(pool_const, 1)
            pool.wait_ge(graph_loaded, 16 * N_GRAPH)
            for k, sign in enumerate((1, -1)):
                g.affine_select(out=a_sem[:, k, :], in_=adjT, compare_op=ALU.is_gt, fill=0.0, base=0,
                                pattern=[[-sign, P]], channel_multiplier=sign).then_inc(pool_const, 1)
            pool.wait_ge(graph_ready, 1)

            def late_constants():
                pool.wait_ge(weights_scaled, 7)
                g.tensor_tensor(a_semL[:, :, :], a_sem[:, :, :], a_semH[:, :, :], ALU.subtract
                                ).then_inc(weights_split, 1)
                for k, p in enumerate((1, 2, 4)):
                    g.tensor_tensor(WihL[:, k, :], WihT[:, p - 1, :], WihH[:, k, :], ALU.subtract
                                    ).then_inc(weights_split, 1)
                g.tensor_tensor(WhhL[:, :], WhhT[:, 0, :], WhhH[:, :], ALU.subtract).then_inc(weights_split, 1)


            def norm_scale(stage, mv_t, rs_t, c, inst, tag):
                wait(pool, stage, "dve", c, "mv" + tag, inst)
                g.tensor_tensor(rs_t[c][:, :], mv_t[c][:, :, 6], half[:, :], ALU.pow
                                ).then_inc(sig[stage, "pool"][c], 1)

            def gate(c, j):
                return gg[c][:, :, j:j + 1].to_broadcast([P, GB, P])

            def front(j, k, c, inst, before):
                done = sig["front", "pool"][c]
                if j == 0:
                    norm_scale("front", mv, rs, c, inst, "0")
                if j in (1, 7):
                    wait(pool, "front", "act", c, ("h0H", "h1H")[j // 7], inst)
                    g.tensor_tensor(hL[c][:, :, :], h[c][:, :, :], hH[c][:, :, :], ALU.subtract).then_inc(done, 1)
                if j == 4 and k == 0:
                    wait(pool, "front", "dve", c, "g", inst)
                    g.tensor_tensor(e0[c][:, :, :], over_b(eb), gate(c, 0), ALU.mult).then_inc(done, 1)
                    g.tensor_tensor(e1[c][:, :, :], over_b(oeb), gate(c, 1), ALU.mult).then_inc(done, 1)
                if j == 4 and k == 1:
                    wait(pool, "front", "pool", c, "e1", inst)
                    g.tensor_tensor(e0[c][:, :, :], e0[c][:, :, :], e1[c][:, :, :], ALU.add).then_inc(done, 1)
                if j == 5:
                    wait(pool, "front", "pool", c, "e01", inst)
                    wait(pool, "front", "act", c, "e2", inst)
                    g.tensor_tensor(e0[c][:, :, :], e0[c][:, :, :], e2[c][:, :, :], ALU.add).then_inc(done, 1)
                if j == 6:
                    norm_scale("front", mv, rs, c, inst, "1")
                    g.tensor_tensor(x1b[c][:, :, :], x1[c][:, :, :], over_b(rows_bc[:, 0, :]), ALU.add
                                    ).then_inc(done, 1)
                if j == 10:
                    norm_scale("front", mv, rs, c, inst, "2")

            def lstm(j, k, c, inst, before):
                p, s = LSTM_STEPS[j // 2]
                if j % 2 and s == p - 1 < MAX_SKIP - 1:
                    last = slice(s, s + (P // p - 1) * p + 1, p)
                    wait(pool, "lstm", "act", c, f"{p}.{s}H", inst)
                    g.tensor_tensor(HL[c][:, :, last], H[c][:, :, last], HH[c][:, :, last], ALU.subtract
                                    ).then_inc(sig["lstm", "pool"][c], 1)
                if (p, s) == (2, 0) and j % 2 and k == 0:
                    wait(pool, "lstm", "act", c, "2.0H", inst)
                    g.tensor_tensor(hsL[c][:, :], hs[c][:, :], hsH[c][:, :], ALU.subtract
                                    ).then_inc(sig["lstm", "pool"][c], 1)
                if j == 3 and k == 1:
                    wait(pool, "front", "dve", c, "x2", inst)
                    wait(pool, "att", "dve", c, "x3", inst - 1)
                    g.tensor_tensor(x2h[c][:, :, :], x2[c][:, :, :], ones[:, 0:1].rearrange("p (o d) -> p o d", o=1)
                                    .to_broadcast([P, GB, P]), ALU.mult).then_inc(sig["lstm", "pool"][c], 1)

            def att(j, k, c, inst, before):
                if j == 0:
                    norm_scale("att", amv, ars, c, inst, "")

            run(pool, "pool", {"front": front, "lstm": lstm, "att": att}, late_from=40, late=late_constants)

        @block.vector
        def _(dve):
            v = nc.vector
            count = [0]

            def link(ins):
                count[0] += 1
                ins.then_inc(dve_const, 1)
                dve.wait_ge(dve_const, count[0])

            link(v.memset(half[:, :], -0.5))
            dve.wait_ge(graph_loaded, 16 * N_GRAPH)
            for src, dst, high, low in ((adjT, a_in, a_inH, a_inL), (adj_n, a_out, a_outH, a_outL)):
                link(v.tensor_scalar(scr[:, :], src[:, :], 0.0, None, ALU.is_gt))
                link(v.scalar_tensor_tensor(out=org[:, :], in0=src[:, :], scalar=0.0, in1=scr[:, :],
                                            op0=ALU.min, op1=ALU.add))
                link(v.tensor_tensor(dst[:, :], org[:, :], adjT, ALU.mult))
                link(v.tensor_copy(high[:, :], dst[:, :]))
                link(v.tensor_tensor(low[:, :], dst[:, :], high[:, :], ALU.subtract))
            dve.wait_ge(pool_const, N_POOL_CONST)
            link(v.tensor_tensor(scr[:, :], adj_n, ident[:, :], ALU.mult))
            link(v.tensor_reduce(diag[:, :], scr[:, :], AX_X, ALU.add))
            dve.wait_ge(pe_const, 2)
            link(v.tensor_copy(rows_bc[:, :, :], bank[1][:, :].rearrange("p (k d) -> p k d", d=P)))
            dve.sem_inc(graph_ready, 1)

            def late_constants():
                link(v.tensor_copy(rest[0:1, 0, :], rows_t[0:1, 4, :]))
                link(v.tensor_copy(rest[0:1, 1, :], bank[0][0:1, 0:P]))
                for term in range(3):
                    link(v.tensor_copy(part[0:1, :, term, :], rest[0:1, :, :]))
                    if term < 2:
                        link(v.tensor_tensor(rest[0:1, :, :], rest[0:1, :, :], part[0:1, :, term, :], ALU.subtract))
                for i in range(3):
                    link(v.tensor_copy(pairs_row[0:1, 0, 3 * i:3 * i + 3, :],
                                       part[0:1, 0, i:i + 1, :].to_broadcast([1, 3, P])))
                for i in range(3):
                    link(v.tensor_copy(pairs_row[0:1, 1, 3 * i:3 * i + 3, :], part[0:1, 1, :, :]))
                dve.sem_inc(pairs_ready, 1)
                link(v.tensor_copy(identb[:, :], ident[:, :]))
                link(v.tensor_scalar(maskb[:, :], adj_n, 0.0, MASKED, ALU.is_equal, ALU.mult))
                dve.wait_ge(weights_loaded, 16 * N_WEIGHTS)
                link(v.tensor_tensor(gb[:, :, :], lb[:, 0, :, :], lb[:, 1, :, :], ALU.add))
                link(v.tensor_scalar(gb[:, :, I:G], gb[:, :, I:G], 0.5, None, ALU.mult))
                link(v.tensor_scalar(gb[:, :, O:O + 1], gb[:, :, O:O + 1], 0.5, None, ALU.mult))
                for k, dst in ((2, attW[:, P:P + 1]), (3, wa2[:, :])):
                    link(v.tensor_tensor(scr[:, :], attW[:, 0:P], rows_bc[:, k, :], ALU.mult))
                    link(v.tensor_reduce(dst, scr[:, :], AX_X, ALU.add))
                link(v.tensor_scalar(wa2_bc[:, :], ones[:, :], wa2[:, 0:1], None, ALU.mult))
                dve.sem_inc(consts_ready, 1)

            def norm_stats(k, stage, src, st_t, mv_t, c, inst, tag, first):
                done = sig[stage, "dve"][c]
                even, odd = st_t[c][:, :, 1:3], st_t[c][:, :, 4:6]
                if k == first:
                    for b in range(GB):
                        ins = v.bn_stats(st_t[c][:, b, :], src[c][:, b, :])
                    ins.then_inc(done, 1)
                if k == first + 1:
                    wait(dve, stage, "dve", c, "st" + tag, inst)
                    v.tensor_tensor(mv_t[c][:, :, 0:2], even, odd, ALU.add).then_inc(done, 1)
                    v.tensor_tensor(mv_t[c][:, :, 2], even[:, :, 0], odd[:, :, 0], ALU.subtract).then_inc(done, 1)
                if k == first + 2:
                    wait(dve, stage, "dve", c, "d" + tag, inst)
                    v.scalar_tensor_tensor(out=mv_t[c][:, :, 3], in0=mv_t[c][:, :, 2], scalar=0.25,
                                           in1=mv_t[c][:, :, 2], op0=ALU.mult, op1=ALU.mult)
                    v.tensor_scalar(mv_t[c][:, :, 4], mv_t[c][:, :, 1], 1.0 / P, EPS, ALU.mult, ALU.add)
                    v.tensor_scalar(mv_t[c][:, :, 5], mv_t[c][:, :, 0], 0.5, None, ALU.mult).then_inc(done, 1)
                if k == first + 3:
                    wait(dve, stage, "dve", c, "dd" + tag, inst)
                    v.tensor_tensor(mv_t[c][:, :, 6], mv_t[c][:, :, 3], mv_t[c][:, :, 4], ALU.add
                                    ).then_inc(done, 1)

            def normed(stage, dst, src, mv_t, rs_t, c, inst, tag):
                wait(dve, stage, "pool", c, "rs" + tag, inst)
                for b in range(GB):
                    ins = v.tensor_scalar(dst[c][:, b, :], src[c][:, b, :], mv_t[c][:, b, 5:6], rs_t[c][:, b:b + 1],
                                          ALU.subtract, ALU.mult)
                ins.then_inc(sig[stage, "dve"][c], 1)

            def gate(c, j):
                return gg[c][:, :, j:j + 1].to_broadcast([P, GB, P])

            def front(j, k, c, inst, before):
                done = sig["front", "dve"][c]
                if j == 0:
                    if k == 0:
                        dve.wait_ge(x_loaded[c], 16 * (inst + 1))
                    norm_stats(k, "front", xin, st, mv, c, inst, "0", first=0)
                if j == 1:
                    normed("front", xn, xin, mv, rs, c, inst, "0")
                if j == 3:
                    wait(dve, "front", "pe", c, "gates", inst)
                    v.tensor_tensor(gz[c][:, :, :], Rb[c][:, 0:3 * GB].rearrange("p (b k) -> p b k", k=3),
                                    gbias.rearrange("p (o k) -> p o k", o=1).to_broadcast([P, GB, 3]),
                                    ALU.add).then_inc(done, 1)
                if j == 4:
                    wait(dve, "front", "act", c, "tanh", inst)
                    v.tensor_scalar(gg[c][:, :, :], gt[c][:, :, :], 0.5, 0.5, ALU.mult, ALU.add).then_inc(done, 1)
                if j == 5 and k == 0:
                    wait(dve, "front", "dve", c, "g", inst)
                    wait(dve, "front", "pe", c, "in", inst)
                    v.tensor_tensor(u1[c][:, :, :], as_b(Ra[c]), gate(c, 0), ALU.mult).then_inc(done, 1)
                if j == 5 and k == 1:
                    wait(dve, "front", "pe", c, "out", inst)
                    v.tensor_tensor(u2[c][:, :, :], as_b(Rb[c]), gate(c, 1), ALU.mult).then_inc(done, 1)
                if j == 5 and k == 2:
                    wait(dve, "front", "dve", c, "u2", inst)
                    v.tensor_tensor(flat(u1[c]), flat(u1[c]), flat(u2[c]), ALU.add).then_inc(done, 1)
                if j == 6 and k == 0:
                    wait(dve, "front", "dve", c, "u", inst)
                    wait(dve, "front", "pool", c, "e", inst)
                    v.tensor_tensor(flat(u1[c]), flat(u1[c]), flat(e0[c]), ALU.add).then_inc(done, 1)
                if j == 6 and k == 1:
                    wait(dve, "front", "dve", c, "s", inst)
                    v.scalar_tensor_tensor(out=flat(x1[c]), in0=flat(u1[c]), scalar=0.0, in1=flat(xin[c]),
                                           op0=ALU.max, op1=ALU.add).then_inc(done, 1)
                if j == 6:
                    if k == 2:
                        wait(dve, "front", "dve", c, "x1", inst)
                    norm_stats(k, "front", x1, st, mv, c, inst, "1", first=2)
                if j == 7:
                    normed("front", xn, x1, mv, rs, c, inst, "1")
                if j in (8, 9):
                    b = 2 * (j - 8) + 1
                    wait(dve, "front", "pe", c, f"z{b}", inst)
                    v.tensor_copy(z[c][:, b, :, :], Rb[c][:, 0:3 * P].rearrange("p (k n) -> p k n", k=3)
                                  ).then_inc(done, 1)
                if j == 10 and k == 0:
                    wait(dve, "front", "pe", c, "sem", inst)
                    wait(dve, "front", "pool", c, "x1b", inst)
                    wait(dve, "lstm", "pool", c, "hold", inst - 1)
                    v.tensor_tensor(flat(x2[c]), Ra[c][:, :], flat(x1b[c]), ALU.add).then_inc(done, 1)
                if j == 10:
                    if k == 1:
                        wait(dve, "front", "dve", c, "x2", inst)
                    norm_stats(k, "front", x2, st, mv, c, inst, "2", first=1)
                if j == 11:
                    normed("front", xn, x2, mv, rs, c, inst, "2")

            def gcn(j, k, c, inst, before):
                done = sig["gcn", "dve"][c]
                if j == 2:
                    wait(dve, "gcn", "pe", c, "w1", inst)
                    v.tensor_tensor(y1[c], as_b(La[c]), over_b(rows_bc[:, 1, :]), ALU.add
                                    ).then_inc(done, 1)
                if j == 3:
                    wait(dve, "gcn", "act", c, "hin", inst)
                    v.scalar_tensor_tensor(out=flat(hinL[c]), in0=Lb[c][:, :], scalar=0.0, in1=flat(hinH[c]),
                                           op0=ALU.max, op1=ALU.subtract).then_inc(done, 1)

            def lstm(j, k, c, inst, before):
                done = sig["lstm", "dve"][c]
                p, s = LSTM_STEPS[j // 2]
                at, n = f"{p}.{s}", GB * (P // p)
                if j % 2 == 0:
                    if k == 0:
                        wait(dve, "lstm", "act", c, at + "g", inst)
                        v.scalar_tensor_tensor(out=(ig if s else c2)[c][:, 0:n], in0=ti[c][:, 0:n], scalar=1.0,
                                               in1=tg[c][:, 0:n], op0=ALU.add, op1=ALU.mult).then_inc(done, 1)
                    if k == 1:
                        wait(dve, "lstm", "act", c, at + "f", inst)
                        v.scalar_tensor_tensor(out=fc[c][:, 0:n], in0=tf[c][:, 0:n], scalar=1.0,
                                               in1=c2[c][:, 0:n], op0=ALU.add, op1=ALU.mult).then_inc(done, 1)
                    if k == 2:
                        wait(dve, "lstm", "dve", c, at + "fc", inst)
                        v.scalar_tensor_tensor(out=c2[c][:, 0:n], in0=fc[c][:, 0:n], scalar=0.5,
                                               in1=ig[c][:, 0:n], op0=ALU.mult, op1=ALU.add).then_inc(done, 1)
                else:
                    wait(dve, "lstm", "act", c, at + "tc", inst)
                    if p == 1:
                        wait(dve, "att", "pe", c, "h", inst - 1)
                    a, b = to[c][:, 0:n], tc[c][:, 0:n]
                    if s < p - 1:
                        dst = hs[c][:, 0:n]
                    else:
                        if p > 1:
                            wait(dve, "lstm", "pool", c, f"{p - 1}.{p - 2}L", inst)
                        dst = H[c][:, :, s:s + (P // p - 1) * p + 1:p]
                        a, b = (t.rearrange("p (b w) -> p b w", b=GB) for t in (a, b))
                    v.scalar_tensor_tensor(out=dst, in0=a, scalar=1.0, in1=b, op0=ALU.add, op1=ALU.mult
                                           ).then_inc(done, 1)

            def att(j, k, c, inst, before):
                done = sig["att", "dve"][c]
                if j == 0 and k == 0:
                    wait(dve, "att", "pe", c, "h", inst)
                    wait(dve, "lstm", "pool", c, "hold", inst)
                    v.scalar_tensor_tensor(out=flat(x3[c]), in0=Ra[c][:, :], scalar=0.5, in1=flat(x2h[c]),
                                           op0=ALU.mult, op1=ALU.add).then_inc(done, 1)
                if j == 0:
                    if k == 1:
                        wait(dve, "att", "dve", c, "x3", inst)
                    norm_stats(k, "att", x3, ast, amv, c, inst, "", first=1)
                if j == 1:
                    normed("att", axn, x3, amv, ars, c, inst, "")
                if j == 3:
                    wait(dve, "att", "pe", c, "wh23", inst)
                    v.tensor_copy(wh[c][:, 2:4, 0:P + 1], Rb[c][:, 0:2 * (P + 1)].rearrange("p (b k) -> p b k", b=2)
                                  ).then_inc(done, 1)
                if j == 4 and k == 0:
                    wait(dve, "att", "act", c, "wh", inst)
                    wait(dve, "att", "dve", c, "wh", inst)
                    wait(dve, "att", "pe", c, "z", inst)
                    v.tensor_tensor(ee[c][:, :, :], as_b(Ra[c]), wh[c][:, :, P:P + 1].to_broadcast([P, GB, P]),
                                    ALU.add).then_inc(done, 1)
                if j == 4 and k == 1:
                    wait(dve, "att", "dve", c, "ee", inst)
                    v.scalar_tensor_tensor(out=flat(pr[c]), in0=flat(ee[c]), scalar=ALPHA, in1=flat(ee[c]),
                                           op0=ALU.mult, op1=ALU.max).then_inc(done, 1)
                    v.tensor_reduce(n0[c][:, :], ee[c][:, :, :], AX_X, ALU.max, negate=True).then_inc(done, 1)
                if j == 4 and k == 2:
                    wait(dve, "att", "dve", c, "n0", inst)
                    v.scalar_tensor_tensor(out=nm[c][:, :], in0=n0[c][:, :], scalar=ALPHA, in1=n0[c][:, :],
                                           op0=ALU.mult, op1=ALU.min).then_inc(done, 1)
                if j == 7 and k < 2:
                    wait(dve, "att", "pe", c, ("num01", "num23")[k], inst)
                    v.reciprocal(rc[c][:, 2 * k:2 * k + 2, :], (Ra, Rb)[k][c][:, 0:2 * (P + 2)]
                                 .rearrange("p (b k) -> p b k", b=2)[:, :, P + 1:P + 2]).then_inc(done, 1)
                if j == 7 and k == 2:
                    wait(dve, "att", "dve", c, "r23", inst)
                    dve.wait_ge(out_free[c], 16 * (inst + 1))
                    for b in range(GB):
                        R = (Ra, Rb)[b // 2][c][:, b % 2 * (P + 2):b % 2 * (P + 2) + P]
                        ins = v.scalar_tensor_tensor(out=xo[c][:, b, :], in0=R, scalar=rc[c][:, b, 0:1],
                                                     in1=x3[c][:, b, :], op0=ALU.mult, op1=ALU.add)
                    ins.then_inc(done, 1)

            run(dve, "dve", {"front": front, "gcn": gcn, "lstm": lstm, "att": att}, late_from=100, late=late_constants)

        @block.scalar
        def _(act):
            a = nc.scalar.activation
            for dst, src in (
                (mats[:, :, :], sem_gcn_w.rearrange("k f o -> f k o")),
                (attW[:, 0:P], att_w), (lb[:, :, :, :], lstm_b.rearrange("k d p g -> d k p g")),
                (WihT[:, :, :], wih_t.rearrange("k d g -> d k g")),
                (WhhT[:, :, :], whh_t.rearrange("k d g -> d k g")),
            ):
                act.dma_start(dst, src).then_inc(weights_loaded, 16)
            act.wait_ge(weights_loaded, 16 * N_WEIGHTS)
            a(WihT[:, 1:, :], WihT[:, 1:, :], ACT.Copy, scale=0.5).then_inc(weights_scaled, 1)
            a(WhhT[:, :, :], WhhT[:, :, :], ACT.Copy, scale=0.5).then_inc(weights_scaled, 1)
            act.wait_ge(weights_scaled, 2)
            for k, p in enumerate((1, 2, 4)):
                a(WihH[:, k, :], WihT[:, p - 1, :], ACT.Copy).then_inc(weights_scaled, 1)
            a(WhhH[:, :], WhhT[:, 0, :], ACT.Copy).then_inc(weights_scaled, 1)
            act.wait_ge(pool_const, N_POOL_CONST)
            a(a_semH[:, :, :], a_sem[:, :, :], ACT.Copy).then_inc(weights_scaled, 1)
            act.wait_ge(graph_ready, 1)

            def late_constants():
                act.wait_ge(consts_ready, 1)


            def front(j, k, c, inst, before):
                done = sig["front", "act"][c]
                if j in (1, 7, 11) and k == 0:
                    tag = {1: "0", 7: "1", 11: "2"}[j]
                    wait(act, "front", "dve", c, "xn" + tag, inst)
                    if j == 1:
                        wait(act, "gcn", "pe", c, "q", inst - 1)
                    a(flat(h[c]), flat(xn[c]), ACT.Relu).then_inc(done, 1)
                if (j, k) in ((1, 1), (7, 2)):
                    a(flat(hH[c]), flat(xn[c]), ACT.Relu).then_inc(done, 1)
                if j == 7 and k == 1:
                    wait(act, "front", "act", c, "h1", inst)
                    a(flat(dh[c]), flat(h[c]), ACT.Copy, scale=diag[:, 0:1]).then_inc(done, 1)
                if j == 2:
                    wait(act, "front", "pe", c, "hT", inst)
                    a(flat(hT[c]), Ra[c][:, :], ACT.Copy).then_inc(done, 1)
                if j == 3:
                    wait(act, "front", "dve", c, "gz", inst)
                    a(gt[c][:, :, :], gz[c][:, :, :], ACT.Tanh, scale=0.5).then_inc(done, 1)
                if j == 4:
                    wait(act, "front", "dve", c, "g", inst)
                    for b in range(GB):
                        ins = a(e2[c][:, b, :], h[c][:, b, :], ACT.Copy, scale=gg[c][:, b, 2:3])
                    ins.then_inc(done, 1)
                if j in (8, 9):
                    b = 2 * (j - 8)
                    wait(act, "front", "pe", c, f"z{b}", inst)
                    a(z[c][:, b, :, :], Ra[c][:, 0:3 * P].rearrange("p (k n) -> p k n", k=3), ACT.Copy
                      ).then_inc(done, 1)

            def gcn(j, k, c, inst, before):
                done = sig["gcn", "act"][c]
                if j == 0:
                    wait(act, "gcn", "pe", c, "q", inst)
                    wait(act, "lstm", "dve", c, "4.3h", inst - 1)
                    a(flat(q[c]), La[c][:, :], ACT.Copy).then_inc(done, 1)
                if j == 1:
                    wait(act, "gcn", "pe", c, "w0", inst)
                    a(flat(y0[c]), Lb[c][:, :], ACT.Relu).then_inc(done, 1)
                if j == 3:
                    wait(act, "gcn", "pe", c, "w2", inst)
                    wait(act, "lstm", "pe", c, "1.0o", inst - 1)
                    a(flat(hinH[c]), Lb[c][:, :], ACT.Relu).then_inc(done, 1)

            def lstm(j, k, c, inst, before):
                done = sig["lstm", "act"][c]
                p, s = LSTM_STEPS[j // 2]
                at, n = f"{p}.{s}", GB * (P // p)

                def gate(dst, src, which):
                    a(dst[c][:, 0:n], src, ACT.Tanh, bias=gb[:, p - 1, which:which + 1],
                      scale=1.0 if which == G else 0.5).then_inc(done, 1)

                if p == 1:
                    if j % 2 == 0 and k == 0:
                        wait(act, "lstm", "pe", c, at + "i", inst)
                        gate(ti, La[c][:, :], I)
                    if j % 2 == 0 and k == 1:
                        wait(act, "lstm", "pe", c, at + "g", inst)
                        gate(tg, Lb[c][:, :], G)
                    if j % 2 and k == 0:
                        wait(act, "lstm", "pe", c, at + "o", inst)
                        gate(to, La[c][:, :], O)
                elif j % 2 == 0:
                    at_0 = s % 2 * n if p == MAX_SKIP else 0
                    at_1 = COLS // 2 + at_0
                    if k == 0:
                        wait(act, "lstm", "pe", c, at + "ig", inst)
                        gate(ti, La[c][:, at_0:at_0 + n], I)
                        gate(tg, La[c][:, at_1:at_1 + n], G)
                    if k == 1:
                        wait(act, "lstm", "pe", c, at + "fo", inst)
                        if s:
                            gate(tf, Lb[c][:, at_0:at_0 + n], F)
                        gate(to, Lb[c][:, at_1:at_1 + n], O)
                if j % 2 and k == (1 if p == 1 else 0):
                    wait(act, "lstm", "dve", c, at + "c", inst)
                    a(tc[c][:, 0:n], c2[c][:, 0:n], ACT.Tanh, scale=0.5).then_inc(done, 1)
                if j % 2 and k == 1 and (p, s) == (2, 0):
                    wait(act, "lstm", "dve", c, at + "h", inst)
                    a(hsH[c][:, :], hs[c][:, 0:n], ACT.Copy).then_inc(done, 1)
                elif j % 2 and k == (2 if p == 1 else 1):
                    last = slice(s, s + (P // p - 1) * p + 1, p)
                    wait(act, "lstm", "dve", c, at + "h", inst)
                    a(HH[c][:, :, last], H[c][:, :, last], ACT.Copy).then_inc(done, 1)

            def att(j, k, c, inst, before):
                done = sig["att", "act"][c]
                if j == 1:
                    wait(act, "att", "dve", c, "xn", inst)
                    a(flat(ah[c]), flat(axn[c]), ACT.Relu).then_inc(done, 1)
                if j == 2:
                    wait(act, "att", "pe", c, "hT", inst)
                    a(flat(ahT[c]), Rb[c][:, :], ACT.Copy).then_inc(done, 1)
                if j == 3:
                    wait(act, "att", "pe", c, "wh01", inst)
                    a(wh[c][:, 0:2, 0:P + 1], Ra[c][:, 0:2 * (P + 1)].rearrange("p (b k) -> p b k", b=2), ACT.Copy
                      ).then_inc(done, 1)
                if j == 5:
                    wait(act, "att", "dve", c, "nm", inst)
                    for b in range(GB):
                        ins = a(ee[c][:, b, :], pr[c][:, b, :], ACT.Exp, bias=nm[c][:, b:b + 1])
                    ins.then_inc(done, 1)
                if j == 6:
                    wait(act, "att", "pe", c, "aT", inst)
                    a(flat(aT[c]), Rb[c][:, :], ACT.Copy).then_inc(done, 1)

            run(act, "act", {"front": front, "gcn": gcn, "lstm": lstm, "att": att}, late_from=110, late=late_constants)

        @block.tensor
        def _(pe):
            mm_ = nc.tensor.matmul
            pe.wait_ge(graph_loaded, 16 * N_GRAPH)
            pe.wait_ge(pool_const, N_POOL_CONST)
            mm_(bank[0][0:1, 0:P], ones[:, 0:1], adjT, start=True, stop=True).then_inc(pe_const, 1)
            mm_(bank[1][:, :], ones[0:1, :], rows_t[0:1, 0:4, :].rearrange("p k d -> p (k d)"), start=True, stop=True
                ).then_inc(pe_const, 1)
            pe.wait_ge(graph_ready, 1)

            def late_constants():
                pe.wait_ge(weights_loaded, 16 * N_WEIGHTS)
                pe.wait_ge(consts_ready, 1)
                pe.wait_ge(pairs_moved, 32)


            def bank_free(c, which, before):
                if before is not None:
                    stage, inst = before
                    who, step = {("front", "a"): ("dve", "x2"), ("front", "b"): ("dve", "z3"),
                                 ("att", "a"): ("dve", "out"), ("att", "b"): ("dve", "out")}[stage, which]
                    wait(pe, stage, who, c, step, inst)

            def front(j, k, c, inst, before):
                done = sig["front", "pe"][c]
                if j == 2:
                    wait(pe, "front", "act", c, "h0", inst)
                    bank_free(c, "a", before)
                    for b in range(GB):
                        ins = nc.tensor.transpose(Ra[c][:, b * P:(b + 1) * P], h[c][:, b, :], ident[:, :])
                    ins.then_inc(done, 1)
                if j == 3:
                    wait(pe, "front", "act", c, "hT", inst)
                    bank_free(c, "b", before)
                    for b in range(GB):
                        ins = mm_(Rb[c][:, 3 * b:3 * b + 3], hT[c][:, b, :], gvec, start=True, stop=True)
                    ins.then_inc(done, 1)
                def split_product(dst, high, low):
                    for m, (w, x_) in enumerate(((high, hH), (low, hH), (high, hL))):
                        if m == 2:
                            wait(pe, "front", "pool", c, "h0L", inst)
                        ins = mm_(dst, w[:, :], flat(x_[c]), start=m == 0, stop=m == 2)
                    ins.then_inc(done, 1)

                if j == 4 and k == 0:
                    wait(pe, "front", "act", c, "h0H", inst)
                    split_product(Ra[c][:, :], a_inH, a_inL)
                if j == 4 and k == 1:
                    wait(pe, "front", "dve", c, "gz", inst)
                    split_product(Rb[c][:, :], a_outH, a_outL)
                if j in (8, 9):
                    for b, R in {8: ((0, Ra), (1, Rb)), 9: ((2 + k, (Ra, Rb)[k]),)}[j]:
                        if b == 0:
                            if isinstance(inst, int) and inst == 0:
                                pe.wait_ge(weights_split, 1)
                            wait(pe, "front", "act", c, "h1H", inst)
                        if b == 2:
                            wait(pe, "front", "act", c, "z0", inst)
                        if b == 3:
                            wait(pe, "front", "dve", c, "z1", inst)
                        nc.tensor.transpose(R[c][:, 0:P], dh[c][:, b, :], ident[:, :])
                        for m, (x_, w) in enumerate(((hH, a_semH), (hH, a_semL), (hL, a_semH))):
                            if b == 0 and m == 2:
                                wait(pe, "front", "pool", c, "h1L", inst)
                            ins = mm_(R[c][:, P:3 * P], x_[c][:, b, :], w[:, :, :].rearrange("p k n -> p (k n)"),
                                      start=m == 0, stop=m == 2)
                        ins.then_inc(done, 1)
                if j == 10:
                    wait(pe, "front", "act", c, "z2", inst)
                    wait(pe, "front", "dve", c, "z3", inst)
                    for b in range(GB):
                        for k in range(3):
                            ins = mm_(Ra[c][:, b * P:(b + 1) * P], z[c][:, b, k, :], semW[:, k, :],
                                      start=k == 0, stop=k == 2)
                    ins.then_inc(done, 1)

            def gcn(j, k, c, inst, before):
                done = sig["gcn", "pe"][c]
                if j == 0:
                    wait(pe, "front", "act", c, "h2", inst)
                    wait(pe, "lstm", "act", c, "4.3o", inst - 1)
                    for b in range(GB):
                        ins = mm_(La[c][:, b * P:(b + 1) * P], h[c][:, b, :], adjT, start=True, stop=True)
                    ins.then_inc(done, 1)
                if j == 1:
                    wait(pe, "gcn", "act", c, "q", inst)
                    mm_(Lb[c][:, :], Wg[:, 0, :], flat(q[c]), start=True, stop=False)
                    mm_(as_b(Lb[c]), bg0_9[0:9, :], rs_9[0:9, :].rearrange("p (o n) -> p o n", o=1)
                        .to_broadcast([9, GB, P]), start=False, stop=True).then_inc(done, 1)
                if j == 2:
                    wait(pe, "gcn", "act", c, "y0", inst)
                    for b in range(GB):
                        ins = mm_(La[c][:, b * P:(b + 1) * P], y0[c][:, b, :], Wg[:, 1, :], start=True, stop=True)
                    ins.then_inc(done, 1)
                if j == 3:
                    wait(pe, "gcn", "dve", c, "y1", inst)
                    for b in range(GB):
                        ins = mm_(Lb[c][:, b * P:(b + 1) * P], y1[c][:, b, :], adjT, start=True, stop=True)
                    ins.then_inc(done, 1)

            def lstm(j, k, c, inst, before):
                done = sig["lstm", "pe"][c]
                p, s = LSTM_STEPS[j // 2]
                at, nw = f"{p}.{s}", P // p
                n = GB * nw
                def split_products(places, high, low, xH, xL, low_ready=None, closes=True):
                    for which, dst, first in places:
                        mm_(dst, high[:, which * P:(which + 1) * P], xH, start=first, stop=False,
                            skip_group_check=True)
                        mm_(dst, low[:, which * P:(which + 1) * P], xH, start=False, stop=False,
                            skip_group_check=True)
                    if low_ready is not None:
                        low_ready()
                    for which, dst, _ in places:
                        ins = mm_(dst, high[:, which * P:(which + 1) * P], xL, start=False, stop=closes,
                                  skip_group_check=True)
                        if closes and (which in (G, O) or p == 1):
                            ins.then_inc(done, 1)

                if p == 1:
                    if j % 2 == 0:
                        if isinstance(inst, int) and inst == 0:
                            pe.wait_ge(weights_split, 5)
                        wait(pe, "gcn", "act", c, "hin", inst)
                        split_products(((I, La[c][:, :], True),), WihH[:, 0, :], WihL[:, 0, :],
                                       flat(hinH[c]), flat(hinL[c]),
                                       lambda: wait(pe, "gcn", "dve", c, "hinL", inst))
                        split_products(((G, Lb[c][:, :], True),), WihH[:, 0, :], WihL[:, 0, :],
                                       flat(hinH[c]), flat(hinL[c]))
                    else:
                        wait(pe, "lstm", "act", c, at + "i", inst)
                        split_products(((O, La[c][:, :], True),), WihH[:, 0, :], WihL[:, 0, :],
                                       flat(hinH[c]), flat(hinL[c]))
                    return

                def gates(first):
                    at_0 = s % 2 * n if p == MAX_SKIP else 0
                    for which, R, col in ((I, La, 0), (G, La, COLS // 2), (F, Lb, 0), (O, Lb, COLS // 2)):
                        if not (first and which == F):
                            yield which, R[c][:, col + at_0:col + at_0 + n]

                def opens(which, at_s):
                    return which in (I, F) or (which == O and at_s == 0 and p < MAX_SKIP)

                def low_of_x():
                    wait(pe, "lstm", "pool", c, f"{p - 1}.{p - 2}L", inst)

                def from_x(at_s):
                    last = slice(at_s, at_s + (nw - 1) * p + 1, p)
                    places = [(which, dst.rearrange("p (b w) -> p b w", b=GB), opens(which, at_s))
                              for which, dst in gates(at_s == 0)]
                    if p == 2:
                        split_products(places, WihH[:, 1, :], WihL[:, 1, :], HH[c][:, :, last], HL[c][:, :, last],
                                       low_of_x if at_s == 0 else None, closes=at_s == 0)
                        return
                    for which, dst, first in places:
                        ins = mm_(dst, WihT[:, p - 1, which * P:(which + 1) * P], H[c][:, :, last], start=first,
                                  stop=at_s == 0, skip_group_check=True)
                        if at_s == 0 and which in (G, O):
                            ins.then_inc(done, 1)

                def from_x_pair(at_s):
                    xH, xL = (t[c][:, :, :].rearrange("p b (w k) -> p k b w", k=p)[:, at_s:at_s + 2]
                              for t in (HH, HL))
                    places = [(which, R[c][:, col:col + 2 * n].rearrange("p (k b w) -> p k b w", k=2, b=GB),
                               which in (I, F))
                              for which, R, col in ((I, La, 0), (G, La, COLS // 2), (F, Lb, 0), (O, Lb, COLS // 2))]
                    split_products(places, WihH[:, 2, :], WihL[:, 2, :], xH, xL, low_of_x if at_s == 0 else None,
                                   closes=at_s == 0)

                if p == MAX_SKIP and j % 2 == 0 and s == 0:
                    wait(pe, "lstm", "act", c, f"{p - 1}.{p - 2}H", inst)
                    from_x_pair(0)
                elif p == MAX_SKIP and j % 2:
                    if s == 1:
                        wait(pe, "lstm", "act", c, at + "o", inst)
                        from_x_pair(2)
                elif p == 2 and j % 2 == 0 and s == 0:
                    wait(pe, "lstm", "act", c, "1.0H", inst)
                    from_x(0)
                elif j % 2 == 0 and s == 0:
                    wait(pe, "lstm", "dve", c, f"{p - 1}.{p - 2}h", inst)
                    from_x(0)
                elif p == 2 and j % 2 == 0:
                    wait(pe, "lstm", "act", c, "2.0H", inst)
                    split_products([(which, dst, False) for which, dst in gates(False)], WhhH[:, :], WhhL[:, :],
                                   hsH[c][:, :], hsL[c][:, :], lambda: wait(pe, "lstm", "pool", c, "2.0L", inst))
                elif j % 2 == 0:
                    wait(pe, "lstm", "dve", c, f"{p}.{s - 1}h", inst)
                    for which, dst in gates(False):
                        ins = mm_(dst, WhhT[:, p - 2, which * P:(which + 1) * P], hs[c][:, 0:n], start=False,
                                  stop=True, skip_group_check=True)
                        if which in (G, O):
                            ins.then_inc(done, 1)
                elif s + 1 < p:
                    wait(pe, "lstm", "act", c, at + "o", inst)
                    from_x(s + 1)

            def att(j, k, c, inst, before):
                done = sig["att", "pe"][c]
                if j == 0:
                    wait(pe, "lstm", "dve", c, "4.3h", inst)
                    bank_free(c, "a", before)
                    for b in range(GB):
                        ins = nc.tensor.transpose(Ra[c][:, b * P:(b + 1) * P], H[c][:, b, :], ident[:, :])
                    ins.then_inc(done, 1)
                if j == 2:
                    wait(pe, "att", "act", c, "h3", inst)
                    bank_free(c, "b", before)
                    for b in range(GB):
                        ins = nc.tensor.transpose(Rb[c][:, b * P:(b + 1) * P], ah[c][:, b, :], ident[:, :])
                    ins.then_inc(done, 1)
                if j == 3:
                    wait(pe, "att", "act", c, "hT", inst)
                    for R, b0 in ((Ra, 0), (Rb, 2)):
                        for b in (0, 1):
                            ins = mm_(R[c][:, b * (P + 1):(b + 1) * (P + 1)], ahT[c][:, b0 + b, :], attW[:, 0:P + 1],
                                      start=True, stop=True)
                        ins.then_inc(done, 1)
                if j == 4:
                    wait(pe, "att", "act", c, "wh", inst)
                    mm_(Ra[c][:, :], wa2_bc[:, :], flat(ahT[c]), start=True, stop=False)
                    mm_(as_b(Ra[c]), identb[:, :], over_b(maskb[:, :]), start=False, stop=True).then_inc(done, 1)
                if j == 6:
                    wait(pe, "att", "act", c, "p", inst)
                    wait(pe, "att", "dve", c, "wh", inst)
                    for b in range(GB):
                        ins = nc.tensor.transpose(Rb[c][:, b * P:(b + 1) * P], ee[c][:, b, :], ident[:, :])
                    ins.then_inc(done, 1)
                if j == 7:
                    wait(pe, "att", "act", c, "aT", inst)
                    for b in (0, 1):
                        ins = mm_((Ra, Rb)[k][c][:, b * (P + 2):(b + 1) * (P + 2)], aT[c][:, 2 * k + b, :],
                                  wh[c][:, 2 * k + b, :], start=True, stop=True)
                    ins.then_inc(done, 1)

            run(pe, "pe", {"front": front, "gcn": gcn, "lstm": lstm, "att": att}, late_from=100, late=late_constants)


def kernel(**inputs):
    import numpy as np
    import concourse.bacc as bacc
    from concourse.bass_utils import run_bass_kernel_spmd

    t = {name: np.asarray(a) for name, a in inputs.items()}
    lstm_b = [t[f"L2_gnn_{b}"].reshape(MAX_SKIP, 4, P).transpose(2, 0, 1) for b in ("bih", "bhh")]
    arrays = {
        "x": t["x"],
        "graph": np.stack([t["adj"].T, t["adj"], t["L0_gnn_edge_bias"], t["L0_gnn_out_edge_bias"]]),
        "gate_cols": np.concatenate([t["L0_gnn_gate_weight"], t["L0_gnn_out_gate_weight"], t["L0_gnn_loop_gate"],
                                     t["L0_gnn_bias_gate"], t["L0_gnn_out_bias_gate"],
                                     np.zeros((P, 1), np.float32)], axis=1),
        "rows": np.stack([t["L1_gnn_bias"], t["L2_gnn_bg1"], t["L3_gnn_a"][:P, 0], t["L3_gnn_a"][P:, 0],
                          t["L2_gnn_bg0"]])[None],
        "sem_gcn_w": np.concatenate([t["L1_gnn_W"], t["L2_gnn_Wg0"][None], t["L2_gnn_Wg1"][None]]),
        "wih_t": t["L2_gnn_Wih"].transpose(0, 2, 1),
        "whh_t": t["L2_gnn_Whh"][1:].transpose(0, 2, 1),
        "lstm_b": np.stack(lstm_b),
        "att_w": t["L3_gnn_W"],
    }
    arrays = {f"in_{name}": np.ascontiguousarray(a) for name, a in arrays.items()}
    nc = bacc.Bacc("TRN2", target_bir_lowering=False, num_devices=1)
    aps = [nc.dram_tensor(name, a.shape, mybir.dt.from_np(a.dtype), kind="ExternalInput").ap()
           for name, a in arrays.items()]
    out = nc.dram_tensor("out", t["x"].shape, F32, kind="ExternalOutput").ap()
    graph_layers_kernel(nc, *aps, out)
    return run_bass_kernel_spmd(nc, [arrays], core_ids=[0]).results[0]["out"]
```
